# Optimizing a Trainium2 kernel written in Bass

```python
import numpy as np
import jax
import jax.numpy as jnp

def _softmax(x, axis=-1):
    return jax.nn.softmax(x, axis=axis)

def _gelu(x):
    return jax.nn.gelu(x, approximate=True)

def _silu(x):
    return jax.nn.silu(x)

def _sigmoid(x):
    return jax.nn.sigmoid(x)

def _layernorm(x, axis=-1, eps=1e-05):
    m = jnp.mean(x, axis=axis, keepdims=True)
    v = jnp.var(x, axis=axis, keepdims=True)
    return (x - m) / jnp.sqrt(v + eps)

def _scatter_add(tgt, idx, src, axis=0):
    return tgt.at[idx].add(src)

def _segment_sum(src, seg, n):
    return jax.ops.segment_sum(src, seg, n)
kernel_name = 'mk_vit_tower_postln_d1_tok_img768_r4_ded6db'

def setup_inputs(seed: int=0):
    np.random.seed(seed)
    _w = jnp.asarray

    def _rec_inputs():
        import jax
        import jax.numpy as jnp
        _rk = jax.random.key(seed)
        x = -0.00016672 + 0.999947 * jax.random.normal(jax.random.fold_in(_rk, 1), (64, 3, 224, 224), jnp.float32)
        return x
    x = _rec_inputs()

    def _L0_tok_setup():
        import jax, jax.numpy as jnp
        import numpy as np
        B, C, H, W = (64, 3, 96, 96)
        P = 16
        EMBED = 192
        NP = H // P * (W // P)
        PATCH_DIM = C * P * P
        key = jax.random.key(seed)
        kx, kw, kb = jax.random.split(key, 3)
        x = jax.random.normal(kx, (B, C, H, W), dtype=jnp.float32)
        bound = 1.0 / np.sqrt(PATCH_DIM)
        Wp = jax.random.uniform(kw, (EMBED, PATCH_DIM), minval=-bound, maxval=bound, dtype=jnp.float32)
        bp = jax.random.uniform(kb, (EMBED,), minval=-bound, maxval=bound, dtype=jnp.float32)
        return {'x': x, 'Wp': Wp, 'bp': bp}
    _L0_tok_all = _L0_tok_setup()
    _L0_tok_in = {k: v for k, v in _L0_tok_all.items() if k in ('Wp', 'bp')}
    del _L0_tok_all

    def _L0_attn_setup():
        import jax, jax.numpy as jnp
        import numpy as np
        FEATS = 192
        HEAD = 12
        HD = FEATS // HEAD
        key = jax.random.key(seed)
        ks = jax.random.split(key, 10)
        b, n, f = (8, 256, FEATS)
        s = 1.0 / np.sqrt(f)
        return {'x': jax.random.normal(ks[0], (b, n, f), dtype=jnp.float32), 'bias': jnp.zeros((), dtype=jnp.float32), 'Wq': jax.random.normal(ks[1], (f, f), dtype=jnp.float32) * s, 'bq': jnp.zeros((f,), dtype=jnp.float32), 'Wk': jax.random.normal(ks[2], (f, f), dtype=jnp.float32) * s, 'bk': jnp.zeros((f,), dtype=jnp.float32), 'Wv': jax.random.normal(ks[3], (f, f), dtype=jnp.float32) * s, 'bv': jnp.zeros((f,), dtype=jnp.float32), 'Wo': jax.random.normal(ks[4], (f, f), dtype=jnp.float32) * s, 'bo': jnp.zeros((f,), dtype=jnp.float32)}
    _L0_attn_all = _L0_attn_setup()
    _L0_attn_in = {k: v for k, v in _L0_attn_all.items() if k in ('bias', 'Wq', 'bq', 'Wk', 'bk', 'Wv', 'bv', 'Wo', 'bo')}
    del _L0_attn_all

    def _L0_ffn_setup():
        import jax, jax.numpy as jnp
        import numpy as np
        EPS_NORM = 1e-05
        RMS_EPS = 1e-05

        def _l2_normalize(v):
            n = jnp.sqrt(jnp.sum(v * v, axis=-1, keepdims=True))
            return v / jnp.maximum(n, EPS_NORM)

        def _rms_norm(x, weight, eps):
            ms = jnp.mean(x * x, axis=-1, keepdims=True)
            return x * jax.lax.rsqrt(ms + eps) * weight
        key = jax.random.key(seed)
        ks = jax.random.split(key, 6)
        B, T, D = (8, 1024, 192)
        S, F = (64, 768)
        x = jax.random.normal(ks[0], (B, T, D), dtype=jnp.float32)
        slots = 0.02 * jax.random.normal(ks[1], (S, D), dtype=jnp.float32)
        scale = jnp.ones((S,), dtype=jnp.float32)
        fc1_weight = 0.02 * jax.random.normal(ks[2], (S, D, F), dtype=jnp.float32)
        fc1_bias = jnp.zeros((S, F), dtype=jnp.float32)
        fc2_weight = 0.02 * jax.random.normal(ks[3], (S, F, D), dtype=jnp.float32)
        fc2_bias = jnp.zeros((S, D), dtype=jnp.float32)
        norm_weight = jnp.ones((D,), dtype=jnp.float32)
        return {'x': x, 'slots': slots, 'scale': scale, 'fc1_weight': fc1_weight, 'fc1_bias': fc1_bias, 'fc2_weight': fc2_weight, 'fc2_bias': fc2_bias, 'norm_weight': norm_weight}
    _L0_ffn_all = _L0_ffn_setup()
    _L0_ffn_in = {k: v for k, v in _L0_ffn_all.items() if k in ('slots', 'scale', 'fc1_weight', 'fc1_bias', 'fc2_weight', 'fc2_bias', 'norm_weight')}
    del _L0_ffn_all
    return {'x': x, 'L0_tok_Wp': _L0_tok_in['Wp'], 'L0_tok_bp': _L0_tok_in['bp'], 'L0_attn_bias': _L0_attn_in['bias'], 'L0_attn_Wq': _L0_attn_in['Wq'], 'L0_attn_bq': _L0_attn_in['bq'], 'L0_attn_Wk': _L0_attn_in['Wk'], 'L0_attn_bk': _L0_attn_in['bk'], 'L0_attn_Wv': _L0_attn_in['Wv'], 'L0_attn_bv': _L0_attn_in['bv'], 'L0_attn_Wo': _L0_attn_in['Wo'], 'L0_attn_bo': _L0_attn_in['bo'], 'L0_ffn_slots': _L0_ffn_in['slots'], 'L0_ffn_scale': _L0_ffn_in['scale'], 'L0_ffn_fc1_weight': _L0_ffn_in['fc1_weight'], 'L0_ffn_fc1_bias': _L0_ffn_in['fc1_bias'], 'L0_ffn_fc2_weight': _L0_ffn_in['fc2_weight'], 'L0_ffn_fc2_bias': _L0_ffn_in['fc2_bias'], 'L0_ffn_norm_weight': _L0_ffn_in['norm_weight']}

def reference(x, L0_tok_Wp, L0_tok_bp, L0_attn_bias, L0_attn_Wq, L0_attn_bq, L0_attn_Wk, L0_attn_bk, L0_attn_Wv, L0_attn_bv, L0_attn_Wo, L0_attn_bo, L0_ffn_slots, L0_ffn_scale, L0_ffn_fc1_weight, L0_ffn_fc1_bias, L0_ffn_fc2_weight, L0_ffn_fc2_bias, L0_ffn_norm_weight):
    import jax
    import jax.numpy as jnp

    def _L0_tok_ref(x, Wp, bp):
        import jax, jax.numpy as jnp
        import numpy as np
        B, C, H, W = (64, 3, 96, 96)
        P = 16
        EMBED = 192
        NP = H // P * (W // P)
        PATCH_DIM = C * P * P
        Bx, Cx, Hx, Wx = x.shape
        hp, wp = (Hx // P, Wx // P)
        patches = x.reshape(Bx, Cx, hp, P, wp, P)
        patches = patches.transpose(0, 2, 4, 1, 3, 5)
        patches = patches.reshape(Bx, hp * wp, Cx * P * P)
        return jnp.einsum('bnd,ed->bne', patches, Wp) + bp

    def _L0_attn_ref(x, bias, Wq, bq, Wk, bk, Wv, bv, Wo, bo):
        import jax, jax.numpy as jnp
        import numpy as np
        FEATS = 192
        HEAD = 12
        HD = FEATS // HEAD
        b, n, f = x.shape
        sqrt_d = jnp.sqrt(jnp.asarray(f, dtype=x.dtype))

        def split_heads(t):
            return t.reshape(b, n, HEAD, HD).transpose(0, 2, 1, 3)
        q = split_heads(x @ Wq.T + bq)
        k = split_heads(x @ Wk.T + bk)
        v = split_heads(x @ Wv.T + bv)
        score = jax.nn.sigmoid(jnp.einsum('bhif,bhjf->bhij', q, k) / sqrt_d + bias)
        attn = jnp.einsum('bhij,bhjf->bihf', score, v)
        o = attn.reshape(b, n, f) @ Wo.T + bo
        return o

    def _L0_ffn_ref(x, slots, scale, fc1_weight, fc1_bias, fc2_weight, fc2_bias, norm_weight):
        import jax, jax.numpy as jnp
        import numpy as np
        EPS_NORM = 1e-05
        RMS_EPS = 1e-05

        def _l2_normalize(v):
            n = jnp.sqrt(jnp.sum(v * v, axis=-1, keepdims=True))
            return v / jnp.maximum(n, EPS_NORM)

        def _rms_norm(x, weight, eps):
            ms = jnp.mean(x * x, axis=-1, keepdims=True)
            return x * jax.lax.rsqrt(ms + eps) * weight
        xn = _rms_norm(x, norm_weight, RMS_EPS)
        tok = _l2_normalize(xn)
        sl = _l2_normalize(slots) * scale[:, None]
        logits = jnp.einsum('sd,btd->bst', sl, tok)
        dispatch_w = jax.nn.softmax(logits, axis=-1)
        combine_w = jax.nn.softmax(logits, axis=-2)
        y = jnp.einsum('btd,bst->bsd', xn, dispatch_w)
        y = jnp.einsum('sio,bsi->bso', fc1_weight, y) + fc1_bias
        y = jax.nn.gelu(y, approximate=False)
        y = jnp.einsum('sio,bsi->bso', fc2_weight, y) + fc2_bias
        out = jnp.einsum('bsd,bst->btd', y, combine_w)
        return out
    h = _L0_tok_ref(x, L0_tok_Wp, L0_tok_bp)
    h = _layernorm(h + _L0_attn_ref(h, L0_attn_bias, L0_attn_Wq, L0_attn_bq, L0_attn_Wk, L0_attn_bk, L0_attn_Wv, L0_attn_bv, L0_attn_Wo, L0_attn_bo), axis=-1)
    h = _layernorm(h + _L0_ffn_ref(h, L0_ffn_slots, L0_ffn_scale, L0_ffn_fc1_weight, L0_ffn_fc1_bias, L0_ffn_fc2_weight, L0_ffn_fc2_bias, L0_ffn_norm_weight), axis=-1)
    return h

_drawn_inputs = setup_inputs


def setup_inputs(seed=0):
    import zlib

    import numpy as np

    out = dict(_drawn_inputs(seed))
    spreads = {'L0_attn_bq': (0.0, 0.8),
     'L0_attn_bk': (0.0, 0.8),
     'L0_attn_bv': (0.0, 0.1),
     'L0_attn_bo': (0.0, 0.8),
     'L0_ffn_scale': (1.0, 0.6),
     'L0_ffn_fc1_bias': (0.0, 0.8),
     'L0_ffn_fc2_bias': (0.0, 0.69),
     'L0_ffn_norm_weight': (1.0, 0.6)}
    factors = {'L0_ffn_slots': 8.0, 'L0_ffn_fc1_weight': 5.662, 'L0_ffn_fc2_weight': 4.646}
    for name, (base, spread) in spreads.items():
        noise = np.random.default_rng([zlib.crc32(name.encode()), seed]).standard_normal(out[name].shape)
        drawn = base * np.exp(spread * noise) if base else spread * noise
        out[name] = jnp.asarray(drawn.astype(out[name].dtype))
    for name, factor in factors.items():
        out[name] = (out[name] * factor).astype(out[name].dtype)
    return out
```

```python
from contextlib import ExitStack
from collections import namedtuple

import concourse.bass as bass
from concourse import mybir

F32 = mybir.dt.float32
ALU = mybir.AluOpType
ACT = mybir.ActivationFunctionType
AX_X = mybir.AxisListType.X

NB, NTOK, D = 64, 196, 192
PATCH = 768
HEADS, HD = 12, 16
NS, F = 64, 768
TT = 2
TP = NTOK // TT
KT = 2
KP = D // KT
PK = PATCH // 128
FK = F // 128
HPT = HEADS // KT
PAIRS = HEADS // 2
HALF = PAIRS // 2
EPS = 1e-5
BANK = 512
SBUF_WORDS = 53200
NPAIR = NS // 2

At = namedtuple("At", "n half par")


def nxt(b):
    return At(b.n + 1, b.half + b.par % 2, (b.par + 1) % 2)


def prv(b):
    return At(b.n - 1, b.half - 1 + b.par % 2, (b.par + 1) % 2)


def at(n):
    return At(n, n // 2, n % 2)


def later(b, n):
    return not isinstance(b.n, int) or b.n >= n


def apart(engine, done, value):
    engine.wait_ge(done, value)


SLOTS_AT = 16
RING = 4
Ringed = namedtuple("Ringed", "n half par ring")


class Step:

    def __init__(self, i, u):
        self.i, self.u = i, u

    def has(self, lag):
        return not isinstance(self.i, int) or 0 <= RING * self.i + self.u - lag < NB

    def back(self, lag):
        n = self.u - lag
        return Ringed(RING * self.i + n, 2 * self.i + n // 2, n % 2, n % RING)


def route(engine, step):
    for u in range(-1, RING):
        step(Step(0, u))
    with engine.Fori(1, NB // RING - 1) as i:
        for u in range(RING):
            step(Step(i, u))
    for u in range(RING + 3):
        step(Step(NB // RING - 1, u))


class Layout:

    def __init__(self, arena, start):
        self.arena, self.at = arena, start

    def take(self, parts, *dims):
        size = 1
        for d in dims:
            size *= d
        ap = self.arena[0:parts, self.at:self.at + size]
        self.at += size
        assert self.at <= SBUF_WORDS, self.at
        names = "abcde"[:len(dims)]
        if len(dims) > 1:
            kw = {n: d for n, d in zip(names, dims)}
            ap = ap.rearrange(f"p ({' '.join(names)}) -> p {' '.join(names)}", **kw)
        return ap


def vit_tower(nc, x, wp, bp, attn_bias, wq, bq, wk, bk, wv, bv, wo, bo, slots, scale, w1, b1, w2, b2,
              norm_w, norm_c, ident_d, mask_d, out):
    y2_dram = nc.dram_tensor("slot_outputs", (NB, NS, D), F32, kind="Internal").ap()

    with ExitStack() as ctx:
        def sem(name):
            return ctx.enter_context(nc.semaphore(name))

        arena = ctx.enter_context(nc.sbuf_tensor("arena", [128, SBUF_WORDS], F32))
        psum = ctx.enter_context(nc.psum_tensor("psum", [128, 8 * BANK], F32))

        def bank(i, n=1):
            return psum[:, i * BANK:(i + n) * BANK]

        keep = Layout(arena, 0)
        res = keep.take(TP, NB * TT, D)
        ident = keep.take(128, 128)
        headmask = keep.take(KP, HPT)
        abias = keep.take(TP, 1)
        bp_c, bq_c, bk_c, nw_c = (keep.take(KP, KT) for _ in range(4))
        slwT = keep.take(KP, KT, NS)
        tables_at = keep.at
        tab = Layout(arena, tables_at)
        mv = tab.take(TP, NB * TT, 2)
        ssu = tab.take(TP, NB * TT)
        rstd, nmr, rms, lcoef, tmp = (tab.take(TP, NB * TT) for _ in range(5))
        slot_rows = tab.take(NS, D)
        slot_sq = tab.take(NS, D)
        slot_s = tab.take(NS, 4)
        y_words, c_words, w_words = KT * NB * NS, NPAIR * NTOK, 2 * KT * F + 2 * FK * D
        big_at = SBUF_WORDS - (y_words + c_words + 2 * w_words)
        big = Layout(arena, big_at)
        comb = big.take(128, NPAIR, NTOK)
        yT = big.take(KP, KT, NB, NS)
        w_at = big.at
        w1_s, w2_s = [], []
        for _ in range(2):
            w1_s.append(big.take(KP + 1, 2, KT, F))
            w2_s.append(big.take(128, 2, FK, D))
        assert tab.at <= big_at

        p1 = Layout(arena, big_at)
        xs = [p1.take(128, PK, NTOK) for _ in range(2)]
        wp_s = p1.take(128, PK, D)
        wq_s, wk_s, wv_s, wo_s = (p1.take(KP, KT, D) for _ in range(4))
        hT = p1.take(KP, KT, NTOK)
        qT = [p1.take(KP, KT, NTOK) for _ in range(2)]
        kT = p1.take(KP, KT, NTOK)
        kM = [p1.take(KP, HEADS, NTOK) for _ in range(2)]
        vz = [p1.take(TP, TT, PAIRS * 4, HD) for _ in range(2)]
        sig = p1.take(TP, PAIRS, 2, TT, NTOK)
        aT = p1.take(KP, KT, NTOK)
        hb = [p1.take(TP, TT, D) for _ in range(2)]
        bv_b, bo_b, nw_b = (p1.take(TP, TT, D) for _ in range(3))
        rt = [p1.take(TP, TT, D) for _ in range(2)]
        ut = p1.take(TP, TT, D)
        junk = p1.take(TP, D)
        st = p1.take(TP, TT, 6)
        mvt = [p1.take(TP, TT, 2) for _ in range(2)]
        sst = [p1.take(TP, TT) for _ in range(2)]

        p2 = Layout(arena, w_at + w_words)
        h1s = [p2.take(TP, TT, D) for _ in range(4)]
        hT2 = [p2.take(KP, KT, NTOK) for _ in range(2)]
        zl = [p2.take(TP, TT, NS) for _ in range(2)]
        zm = [p2.take(TP, TT, NS) for _ in range(2)]
        ez = [p2.take(TP, TT, NS) for _ in range(2)]
        en = [p2.take(TP, TT, NS) for _ in range(2)]
        pt = [p2.take(NS, NTOK) for _ in range(2)]
        pn = [p2.take(NS, NTOK) for _ in range(2)]
        dr = [p2.take(TP, TT, NS) for _ in range(2)]
        mx2, sm2, rc2 = (p2.take(TP, TT) for _ in range(3))
        mxt, nmt, zt, rzt = (p2.take(NS, 1) for _ in range(4))

        p3 = Layout(arena, tables_at)
        hid = p3.take(128, F)
        hidT = p3.take(128, FK, 128)
        yst = [p3.take(KP + 1, KT, 2, NB) for _ in range(2)]
        b2_s = [p3.take(128, D) for _ in range(2)]
        y2o = [p3.take(128, D) for _ in range(2)]
        assert p3.at <= big_at

        p4 = Layout(arena, big_at + c_words)
        y2s = [p4.take(128, D) for _ in range(2)]
        cst = [p4.take(128, NTOK) for _ in range(2)]
        rf = [p4.take(TP, 4, D) for _ in range(2)]
        ob = [p4.take(TP, 4, D) for _ in range(2)]
        st4 = p4.take(TP, 4, 6)
        mv4 = [p4.take(TP, 4, 2) for _ in range(2)]
        ve4, sd4 = ([p4.take(TP, 4) for _ in range(2)] for _ in range(2))
        rs4, nm4 = ([p4.take(TP, 4) for _ in range(2)] for _ in range(2))

        ps_sc = [bank(0, 2).rearrange("p (h n) -> p h n", h=2), bank(2, 2).rearrange("p (h n) -> p h n", h=2)]
        ps_av, ps_x, ps_y, ps_z = bank(4), bank(5), bank(6), bank(7)

        def tiles(b, p, n):
            return b[0:p, 0:2 * n].rearrange("p (t n) -> p t n", t=2)

        const_in = sem("const_in")
        x_in = [sem("x_in0"), sem("x_in1")]
        (tok_done, hT_ready, q_done, k_done, qT_ready, kT_ready, kM_ready, v_done, v_ready, tr_done,
         hb_ready, sc_done, sig_done, av_done, aT_ready, o_done, r_ready, st_ready, mv_ready, u_ready,
         ss_ready, kept) = (sem(n) for n in (
             "tok_done", "hT_ready", "q_done", "k_done", "qT_ready", "kT_ready", "kM_ready", "v_done",
             "v_ready", "tr_done", "hb_ready", "sc_done", "sig_done", "av_done", "aT_ready", "o_done",
             "r_ready", "st_ready", "mv_ready", "u_ready", "ss_ready", "kept"))
        vz_zero = sem("vz_zero")
        tables_dve, tables_act, slT_done, slwT_ready = (sem(n) for n in (
            "tables_dve", "tables_act", "slT_done", "slwT_ready"))
        (h1_ready, h1_kept, hT2_done, hT2_ready, lg_done, z_ready, mx_ready, zm_ready, ez_ready, sm_ready,
         rc_ready, en_ready, zT_done, mxt_ready, nmt_ready, pt_ready, rzt_ready, pn_ready, d_done,
         dr_ready, e_done, comb_ready, y_done, yT_ready) = (sem(n) for n in (
             "h1_ready", "h1_kept", "hT2_done", "hT2_ready", "lg_done", "z_ready", "mx_ready", "zm_ready",
             "ez_ready", "sm_ready", "rc_ready", "en_ready", "zT_done", "mxt_ready", "nmt_ready",
             "pt_ready", "rzt_ready", "pn_ready", "d_done", "dr_ready", "e_done", "comb_ready", "y_done",
             "yT_ready"))
        w1_in = [sem("w1_in0"), sem("w1_in1")]
        w2_in = [sem("w2_in0"), sem("w2_in1")]
        b2_in = [sem("b2_in0"), sem("b2_in1")]
        (yst_ready, ones_set, fc1_done, hid_ready, hidT_done, hidT_ready, fc2_done, y2_ready) = (
            sem(n) for n in ("yst_ready", "ones_set", "fc1_done", "hid_ready", "hidT_done", "hidT_ready",
                             "fc2_done", "y2_ready"))
        y2_out = [sem("y2_out0"), sem("y2_out1")]
        y2_in = [sem("y2_in0"), sem("y2_in1")]
        (cst_ready, cm_done, rf_ready, st4_ready, mv4_ready, ve4_ready, sd4_ready, rs4_ready,
         nm4_ready, ob_ready) = (sem(n) for n in ("cst_ready", "cm_done", "rf_ready", "st4_ready", "mv4_ready",
                                       "ve4_ready", "sd4_ready", "rs4_ready", "nm4_ready",
                                       "ob_ready"))
        out_done = [sem("out_done0"), sem("out_done1")]

        consts = [
            (wp_s, wp), (bp_c, bp), (wq_s, wq), (bq_c, bq), (wk_s, wk), (bk_c, bk), (headmask, mask_d),
            (wv_s, wv), (wo_s, wo), (ident, ident_d), (nw_c, norm_c),
            (abias, attn_bias.to_broadcast([TP, 1])),
            (slot_rows, slots), (slot_s[:, 3:4], scale),
        ]
        for tile, row in ((bv_b, bv), (bo_b, bo), (nw_b, norm_w)):
            for t in range(TT):
                consts.append((tile[:, t, :], row.rearrange("(a d) -> a d", a=1).to_broadcast([TP, D])))
        CONSTS = 16 * len(consts)

        out_v = out.rearrange("b (t p) d -> p (b t) d", p=TP)
        block = ctx.enter_context(nc.Block())

        @block.sync
        def _(sp):
            def load_x(b, fresh=False):
                if not fresh:
                    sp.wait_ge(tok_done, b.n - 1)
                sp.dma_start(xs[b.par], x[bass.ds(b.n, 1)].rearrange("a p k n -> (a p) k n")
                             ).then_inc(x_in[b.par], 16)

            for n in range(2):
                sp.dma_start(xs[n], x[n]).then_inc(x_in[n], 16)
                for tile, src in (consts[0:7] if n == 0 else consts[7:]):
                    sp.dma_start(tile, src).then_inc(const_in, 16)
            with sp.Fori(1, NB // 2) as i:
                load_x(At(2 * i, i, 0))
                load_x(At(2 * i + 1, i, 1))

            def load_w1(j):
                if later(j, 2):
                    sp.wait_ge(fc1_done, j.n - 1)
                w1_t = w1_s[j.par]
                sp.dma_start(w1_t[0:KP].rearrange("p s k f -> p s (k f)"),
                             w1[bass.ds(2 * j.n, 2)].rearrange("s p k f -> p s (k f)")).then_inc(w1_in[j.par], 16)
                sp.dma_start(w1_t[KP:KP + 1, :, KT - 1, :],
                             b1[bass.ds(2 * j.n, 2)].rearrange("(a s) f -> a s f", a=1)).then_inc(w1_in[j.par], 16)

            def load_w2(j):
                if later(j, 2):
                    sp.wait_ge(fc2_done, j.n - 1)
                sp.dma_start(w2_s[j.par].rearrange("p s k d -> p s (k d)"),
                             w2[bass.ds(2 * j.n, 2)].rearrange("s p k d -> p s (k d)")).then_inc(w2_in[j.par], 16)

            def load_b2(j):
                if later(j, 2):
                    sp.wait_ge(y2_ready, j.n - 1)
                for s in range(2):
                    sp.dma_start(b2_s[j.par][64 * s:64 * s + 64, :],
                                 b2[bass.ds(2 * j.n + s, 1), :].to_broadcast([NB, D])).then_inc(b2_in[j.par], 16)

            def store_y2(j):
                sp.wait_ge(y2_ready, j.n + 1)
                for s in range(2):
                    sp.dma_start(y2_dram[:, bass.ds(2 * j.n + s, 1), :].rearrange("b a d -> (b a) d"),
                                 y2o[j.par][64 * s:64 * s + 64, :]).then_inc(y2_out[j.par], 16)

            sp.wait_ge(kept, 3 * NB)
            load_w1(at(0))
            load_w2(at(0))
            sp.wait_ge(yT_ready, NB)
            sp.wait_ge(comb_ready, NB)
            sp.wait_ge(h1_kept, NB)
            load_b2(at(0))
            load_w1(at(1))
            load_w2(at(1))
            load_b2(at(1))
            with sp.Fori(0, NPAIR // 2 - 1) as i:
                for u in range(2):
                    j = At(2 * i + u, i, u)
                    load_w1(At(2 * i + u + 2, i + 1, u))
                    load_w2(At(2 * i + u + 2, i + 1, u))
                    load_b2(At(2 * i + u + 2, i + 1, u))
                    store_y2(j)
            for n in (NPAIR - 2, NPAIR - 1):
                store_y2(at(n))

            for s in y2_out:
                sp.wait_ge(s, 32 * (NPAIR // 2))

            def load_y2(i):
                sp.dma_start(y2s[i.par], y2_dram[bass.ds(2 * i.n, 2)].rearrange("b s d -> (b s) d")
                             ).then_inc(y2_in[i.par], 16)

            load_y2(at(0))
            load_y2(at(1))
            with sp.Fori(0, NB // 4 - 1) as i:
                for u in range(2):
                    sp.wait_ge(cm_done, 2 * i + u + 1)
                    load_y2(At(2 * i + u + 2, i + 1, u))
            for s in out_done:
                sp.wait_ge(s, 16 * (NB // 4))

        @block.tensor
        def _(pe):
            mm, tr = nc.tensor.matmul, nc.tensor.transpose

            def tok(b, first=False):
                pe.wait_ge(x_in[b.par], 16 * (b.half + 1))
                if not first:
                    pe.wait_ge(v_ready, b.n)
                o = tiles(ps_x, KP, NTOK)
                for m in range(KT):
                    for k in range(PK):
                        last = mm(o[:, m, :], wp_s[:, k, m * KP:(m + 1) * KP], xs[b.par][:, k, :],
                                  start=k == 0, stop=k == PK - 1)
                last.then_inc(tok_done, 1)

            def project(w, bankap, done):
                o = tiles(bankap, KP, NTOK)
                for m in range(KT):
                    for k in range(KT):
                        last = mm(o[:, m, :], w[:, k, m * KP:(m + 1) * KP], hT[:, k, :],
                                  start=k == 0, stop=k == KT - 1)
                last.then_inc(done, 1)

            def qk(b, early=False):
                pe.wait_ge(hT_ready, b.n + 1)
                if not early:
                    pe.wait_ge(r_ready, b.n - 1)
                project(wq_s, ps_y, q_done)
                if not (early and b.n == 0):
                    pe.wait_ge(hb_ready, b.n)
                project(wk_s, ps_z, k_done)

            def by_token(lhs, w, bankap, done):
                o = tiles(bankap, TP, D)
                for t in range(TT):
                    for k in range(KT):
                        last = mm(o[:, t, :], lhs[:, k, t * TP:(t + 1) * TP], w[:, k, :],
                                  start=k == 0, stop=k == KT - 1)
                last.then_inc(done, 1)

            def v_h(b):
                by_token(hT, wv_s, ps_x, v_done)
                pe.wait_ge(kT_ready, b.n + 1)
                o = tiles(ps_z, TP, D)
                for t in range(TT):
                    for k in range(KT):
                        last = tr(o[:, t, k * KP:(k + 1) * KP], hT[:, k, t * TP:(t + 1) * TP],
                                  ident[0:KP, 0:KP])
                last.then_inc(tr_done, 1)

            def scores(b, g, first=False):
                if g == 0:
                    pe.wait_ge(qT_ready, b.n + 1)
                    pe.wait_ge(kM_ready, b.n + 1)
                if not (first and g < 2):
                    pe.wait_ge(sig_done, 6 * b.n + g - 1)
                for a in range(2):
                    h = 2 * g + a
                    for t in range(TT):
                        last = mm(ps_sc[g % 2][0:TP, a, t * NTOK:(t + 1) * NTOK],
                                  kM[b.par][:, h, t * TP:(t + 1) * TP], qT[b.par][:, h // HPT, :],
                                  start=True, stop=True)
                last.then_inc(sc_done, 1)

            def attend(b, half, first=False):
                pe.wait_ge(sig_done, 6 * b.n + 3 * half + 3)
                if half == 0:
                    pe.wait_ge(v_ready, b.n + 1)
                    if not first:
                        pe.wait_ge(aT_ready, b.n)
                for a in range(2):
                    for t in range(TT):
                        for c in range(HALF):
                            g = HALF * half + c
                            vt = vz[b.par][:, t, 4 * g + 2 * a:4 * g + 2 * a + 2, :]
                            last = mm(ps_av[32 * c:32 * c + 32, half * NTOK:(half + 1) * NTOK],
                                      vt.rearrange("p a f -> p (a f)"), sig[:, g, a, t, :],
                                      start=a == 0 and t == 0, stop=a == 1 and t == TT - 1)
                last.then_inc(av_done, 1)

            def o_proj(b):
                pe.wait_ge(aT_ready, b.n + 1)
                by_token(aT, wo_s, ps_y, o_done)

            def step(b, first=False, last=False):
                scores(b, 0, first)
                if not first:
                    attend(prv(b), 1)
                scores(b, 1, first)
                if not last:
                    tok(nxt(b))
                scores(b, 2)
                if not first:
                    o_proj(prv(b))
                scores(b, 3)
                attend(b, 0, first)
                if not last:
                    qk(nxt(b), early=first)
                scores(b, 4)
                if not last:
                    v_h(nxt(b))
                scores(b, 5)

            pe.wait_ge(const_in, CONSTS)
            tok(at(0), first=True)
            qk(at(0), early=True)
            v_h(at(0))
            step(at(0), first=True)
            with pe.Fori(0, NB // 2 - 1) as i:
                step(At(2 * i + 1, i, 1))
                step(At(2 * i + 2, i + 1, 0))
            step(at(NB - 1), last=True)
            attend(at(NB - 1), 1)
            o_proj(at(NB - 1))

            pe.wait_ge(tables_dve, SLOTS_AT)
            pe.wait_ge(r_ready, NB)
            for k in range(KT):
                last = tr(ps_y[0:KP, k * NS:(k + 1) * NS], slot_sq[:, k * KP:(k + 1) * KP], ident[0:NS, 0:NS])
            last.then_inc(slT_done, 1)
            pe.wait_ge(slwT_ready, 1)

            def h_transposed(b):
                pe.wait_ge(h1_ready, b.n + 1)
                if later(b, 1):
                    pe.wait_ge(hT2_ready, b.n)
                o = tiles(bank(0), KP, NTOK)
                for k in range(KT):
                    for t in range(TT):
                        last = tr(o[:, k, t * TP:(t + 1) * TP], h1s[b.ring][:, t, k * KP:(k + 1) * KP],
                                  ident[0:TP, 0:TP])
                last.then_inc(hT2_done, 1)

            def logits(b):
                pe.wait_ge(hT2_ready, b.n + 1)
                if later(b, 1):
                    pe.wait_ge(z_ready, b.n)
                o = tiles(bank(1), TP, NS)
                for t in range(TT):
                    for k in range(KT):
                        last = mm(o[:, t, :], hT2[b.par][:, k, t * TP:(t + 1) * TP], slwT[:, k, :],
                                  start=k == 0, stop=k == KT - 1)
                last.then_inc(lg_done, 1)

            def z_waits(b):
                pe.wait_ge(z_ready, b.n + 1)
                if later(b, 1):
                    pe.wait_ge(pt_ready, b.n)

            def weight_waits(b):
                pe.wait_ge(pn_ready, b.n + 1)
                pe.wait_ge(en_ready, b.n + 1)
                if later(b, 1):
                    pe.wait_ge(dr_ready, b.n)
                    pe.wait_ge(comb_ready, b.n)

            def z_transposed(b):
                for t in range(TT):
                    last = tr(bank(2)[0:NS, t * TP:(t + 1) * TP], zl[b.par][:, t, :], ident[0:TP, 0:TP])
                last.then_inc(zT_done, 1)

            def weights_transposed(b):
                for t in range(TT):
                    last = tr(bank(3)[0:TP, t * NS:(t + 1) * NS], pn[b.par][:, t * TP:(t + 1) * TP],
                              ident[0:NS, 0:NS])
                last.then_inc(d_done, 1)
                for t in range(TT):
                    last = tr(bank(4)[0:NS, t * TP:(t + 1) * TP], en[b.par][:, t, :], ident[0:TP, 0:TP])
                last.then_inc(e_done, 1)

            def slot_inputs(b):
                pe.wait_ge(dr_ready, b.n + 1)
                if later(b, 1):
                    pe.wait_ge(yT_ready, b.n)
                o = tiles(bank(5), KP, NS)
                for k in range(KT):
                    for t in range(TT):
                        last = mm(o[:, k, :], h1s[b.ring][:, t, k * KP:(k + 1) * KP], dr[b.par][:, t, :],
                                  start=t == 0, stop=t == TT - 1)
                last.then_inc(y_done, 1)

            def pe_step(s):
                for lag, stage in ((3, weight_waits), (1, logits), (3, weights_transposed), (0, h_transposed),
                                   (1, z_waits), (3, slot_inputs), (1, z_transposed)):
                    if s.has(lag):
                        stage(s.back(lag))

            route(pe, pe_step)

            pe.wait_ge(yT_ready, NB)
            pe.wait_ge(comb_ready, NB)
            pe.wait_ge(ones_set, 2)

            def fc1(j, fresh=False):
                pe.wait_ge(w1_in[j.par], 32 * (j.half + 1))
                pe.wait_ge(yst_ready, j.n + 1)
                if not fresh:
                    pe.wait_ge(hid_ready, j.n - 1)
                for half in range(2):
                    for k in range(KT):
                        K = KP + 1 if k == KT - 1 else KP
                        for s in range(2):
                            last = mm(bank(2 * j.par + half)[64 * s:64 * s + 64, 0:F // 2],
                                      yst[j.par][0:K, k, s, :],
                                      w1_s[j.par][0:K, s, k, half * (F // 2):(half + 1) * (F // 2)],
                                      start=k == 0, stop=k == KT - 1)
                last.then_inc(fc1_done, 1)

            def hidden_transposed(j):
                pe.wait_ge(hid_ready, j.n + 1)
                if later(j, 1):
                    pe.wait_ge(hidT_ready, j.n)
                for k in range(FK):
                    last = tr(bank(4, 2)[:, k * 128:(k + 1) * 128], hid[:, k * 128:(k + 1) * 128], ident)
                last.then_inc(hidT_done, 1)

            def fc2(j):
                pe.wait_ge(w2_in[j.par], 16 * (j.half + 1))
                pe.wait_ge(hidT_ready, j.n + 1)
                if later(j, 1):
                    pe.wait_ge(y2_ready, j.n)
                for k in range(FK):
                    for s in range(2):
                        last = mm(bank(6)[64 * s:64 * s + 64, 0:D], hidT[:, k, 64 * s:64 * s + 64],
                                  w2_s[j.par][:, s, k, :], start=k == 0, stop=k == FK - 1)
                last.then_inc(fc2_done, 1)

            def expert(j, last=False, fresh=False):
                hidden_transposed(j)
                if not last:
                    fc1(nxt(j), fresh)
                fc2(j)

            fc1(at(0), fresh=True)
            expert(at(0), fresh=True)
            with pe.Fori(0, NPAIR // 2 - 1) as i:
                expert(At(2 * i + 1, i, 1))
                expert(At(2 * i + 2, i + 1, 0))
            expert(at(NPAIR - 1), last=True)

            def combine(i, fresh=False):
                pe.wait_ge(y2_in[i.par], 16 * (i.half + 1))
                pe.wait_ge(cst_ready, i.n + 1)
                if not fresh:
                    pe.wait_ge(rf_ready, i.n - 1)
                for t in range(TT):
                    for e in range(2):
                        last = mm(bank(2 * i.par + e)[0:TP, t * D:(t + 1) * D],
                                  cst[i.par][64 * e:64 * e + 64, t * TP:(t + 1) * TP],
                                  y2s[i.par][64 * e:64 * e + 64, :], start=True, stop=True)
                last.then_inc(cm_done, 1)

            pe.wait_ge(hid_ready, NPAIR)
            combine(at(0), fresh=True)
            combine(at(1), fresh=True)
            with pe.Fori(1, NB // 4) as i:
                combine(At(2 * i, i, 0))
                combine(At(2 * i + 1, i, 1))

        @block.scalar
        def _(act):
            fn = nc.scalar.activation

            def sigmoid(b, g, first=False):
                act.wait_ge(sc_done, 6 * b.n + g + 1)
                if not first:
                    act.wait_ge(av_done, 2 * b.n + g // HALF - 1)
                fn(sig[:, g].rearrange("p a t n -> p a (t n)"), ps_sc[g % 2][0:TP, :, 0:TT * NTOK],
                   ACT.Sigmoid, bias=abias, scale=float(D) ** -0.5).then_inc(sig_done, 1)

            def biased(dst, bankap, bias, ready):
                src = tiles(bankap, KP, NTOK)
                for m in range(KT):
                    last = fn(dst[:, m, :], src[:, m, :], ACT.Identity, bias=bias[:, m:m + 1])
                last.then_inc(ready, 1)

            def h_out(b, first=False):
                act.wait_ge(tok_done, b.n + 1)
                if not first:
                    act.wait_ge(tr_done, b.n)
                biased(hT, ps_x, bp_c, hT_ready)

            def qk_out(b, early=False):
                act.wait_ge(q_done, b.n + 1)
                if not early:
                    act.wait_ge(sc_done, 6 * b.n - 6)
                biased(qT[b.par], ps_y, bq_c, qT_ready)
                act.wait_ge(k_done, b.n + 1)
                if later(b, 1):
                    act.wait_ge(kM_ready, b.n)
                biased(kT, ps_z, bk_c, kT_ready)

            def step(b, first=False, last=False):
                sigmoid(b, 0, first)
                sigmoid(b, 1, first)
                if not last:
                    h_out(nxt(b))
                sigmoid(b, 2, first)
                sigmoid(b, 3, first)
                if not last:
                    qk_out(nxt(b), early=first)
                sigmoid(b, 4, first)
                sigmoid(b, 5, first)

            act.wait_ge(const_in, CONSTS)
            h_out(at(0), first=True)
            qk_out(at(0), early=True)
            step(at(0), first=True)
            with act.Fori(0, NB // 2 - 1) as i:
                step(At(2 * i + 1, i, 1))
                step(At(2 * i + 2, i + 1, 0))
            step(at(NB - 1), last=True)

            act.wait_ge(tables_dve, 1)
            fn(lcoef, tmp, ACT.Sqrt).then_inc(tables_act, 1)
            act.wait_ge(tables_dve, 2)
            fn(slot_s[:, 1:2], slot_s[:, 0:1], ACT.Sqrt).then_inc(tables_act, 1)
            act.wait_ge(tables_dve, 7)
            fn(lcoef, tmp, ACT.Sqrt).then_inc(tables_act, 1)
            fn(ssu, ssu, ACT.Sqrt).then_inc(tables_act, 1)

            def normalise(b):
                if later(b, 4):
                    act.wait_ge(y_done, b.n - 3)
                    act.wait_ge(h1_kept, b.n - 3)
                for t in range(TT):
                    row = bass.ds(2 * b.n + t, 1)
                    last = fn(h1s[b.ring][:, t, :], res[:, row, :].rearrange("p a d -> p (a d)"), ACT.Identity,
                              bias=nmr[:, row], scale=rstd[:, row])
                last.then_inc(h1_ready, 1)

            def hT2_out(b):
                act.wait_ge(hT2_done, b.n + 1)
                if later(b, 2):
                    act.wait_ge(lg_done, b.n - 1)
                fn(hT2[b.par], tiles(bank(0), KP, NTOK), ACT.Identity).then_inc(hT2_ready, 1)

            def exp_slots(b):
                act.wait_ge(zm_ready, b.n + 1)
                if later(b, 2):
                    act.wait_ge(en_ready, b.n - 1)
                fn(ez[b.par], zm[b.par], ACT.Exp).then_inc(ez_ready, 1)

            def exp_tokens(b):
                act.wait_ge(zT_done, b.n + 1)
                act.wait_ge(nmt_ready, b.n + 1)
                if later(b, 1):
                    act.wait_ge(pn_ready, b.n)
                fn(pt[b.par], bank(2)[0:NS, 0:NTOK], ACT.Exp, bias=nmt, accum_out=zt).then_inc(pt_ready, 1)

            def comb_out(b):
                act.wait_ge(e_done, b.n + 1)
                fn(comb[64 * b.par:64 * b.par + 64, bass.ds(b.half, 1), :].rearrange("p a n -> p (a n)"),
                   bank(4)[0:NS, 0:NTOK], ACT.Copy).then_inc(comb_ready, 1)

            def yT_out(b):
                act.wait_ge(y_done, b.n + 1)
                for k in range(KT):
                    last = fn(yT[:, k, bass.ds(b.n, 1), :].rearrange("p a s -> p (a s)"),
                              bank(5)[0:KP, k * NS:(k + 1) * NS], ACT.Copy, scale=nw_c[:, k:k + 1])
                last.then_inc(yT_ready, 1)

            def act_step(s):
                for lag, stage in ((2, exp_tokens), (0, hT2_out), (1, exp_slots), (3, comb_out),
                                   (3, yT_out), (-1, normalise)):
                    if s.has(lag):
                        stage(s.back(lag))

            act.wait_ge(slwT_ready, 1)
            route(act, act_step)

            def gelu(j):
                act.wait_ge(fc1_done, j.n + 1)
                if later(j, 1):
                    act.wait_ge(hidT_done, j.n)
                fn(hid.rearrange("p (h f) -> p h f", h=2),
                   bank(2 * j.par, 2).rearrange("p (h f) -> p h f", h=2)[:, :, 0:F // 2],
                   ACT.Gelu).then_inc(hid_ready, 1)

            gelu(at(0))
            with act.Fori(0, NPAIR // 2 - 1) as i:
                gelu(At(2 * i + 1, i, 1))
                gelu(At(2 * i + 2, i + 1, 0))
            gelu(at(NPAIR - 1))

            def root(i, fresh=False):
                act.wait_ge(ve4_ready, i.n + 1)
                if not fresh:
                    act.wait_ge(rs4_ready, i.n - 1)
                fn(sd4[i.par], ve4[i.par], ACT.Sqrt).then_inc(sd4_ready, 1)

            def final(i, fresh=False):
                act.wait_ge(nm4_ready, i.n + 1)
                if not fresh:
                    act.wait_ge(out_done[i.par], 16 * i.half)
                for t in range(4):
                    last = fn(ob[i.par][:, t, :], rf[i.par][:, t, :], ACT.Identity, bias=nm4[i.par][:, t:t + 1],
                              scale=rs4[i.par][:, t:t + 1])
                last.then_inc(ob_ready, 1)
                act.wait_ge(ob_ready, i.n + 1)
                act.dma_start(out_v[:, bass.ds(4 * i.n, 4), :], ob[i.par]).then_inc(out_done[i.par], 16)

            root(at(0), True)
            root(at(1), True)
            final(at(0), True)
            root(at(2))
            final(at(1), True)
            with act.Fori(1, NB // 4 - 1) as i:
                root(At(2 * i + 1, i, 1))
                final(At(2 * i, i, 0))
                root(At(2 * i + 2, i + 1, 0))
                final(At(2 * i + 1, i, 1))
            root(at(NB // 2 - 1))
            final(at(NB // 2 - 2))
            final(at(NB // 2 - 1))

        @block.gpsimd
        def _(pool):
            copy = nc.gpsimd.tensor_copy
            for v in vz:
                last = nc.gpsimd.memset(v, 0.0)
            last.then_inc(vz_zero, 1)

            def keep_rows(b):
                pool.wait_ge(r_ready, b.n + 1)
                copy(res[:, bass.ds(2 * b.n, 2), :], rt[b.par]).then_inc(kept, 1)
                pool.wait_ge(mv_ready, b.n + 1)
                copy(mv[:, bass.ds(2 * b.n, 2), :], mvt[b.par]).then_inc(kept, 1)
                pool.wait_ge(ss_ready, b.n + 1)
                copy(ssu[:, bass.ds(2 * b.n, 2)], sst[b.par]).then_inc(kept, 1)

            with pool.Fori(0, NB // 2) as i:
                keep_rows(At(2 * i, i, 0))
                keep_rows(At(2 * i + 1, i, 1))

            with pool.Fori(0, NB // 4) as i:
                for u in range(4):
                    pool.wait_ge(h1_ready, 4 * i + u + 1)
                    copy(res[:, bass.ds(8 * i + 2 * u, 2), :], h1s[u]).then_inc(h1_kept, 1)

            pool.wait_ge(yT_ready, NB)
            pool.wait_ge(comb_ready, NB)
            pool.wait_ge(h1_kept, NB)
            for n, y in enumerate(yst):
                nc.gpsimd.memset(y[KP:KP + 1], 1.0).then_inc(ones_set, 1)
                pool.wait_ge(ones_set, n + 1)

            def stage_y(j, fresh=False):
                if not fresh:
                    pool.wait_ge(fc1_done, j.n - 1)
                for k in range(KT):
                    last = copy(yst[j.par][0:KP, k], yT[:, k, :, bass.ds(2 * j.n, 2)].rearrange("p b s -> p s b"))
                last.then_inc(yst_ready, 1)

            stage_y(at(0), True)
            stage_y(at(1), True)
            with pool.Fori(1, NPAIR // 2) as i:
                stage_y(At(2 * i, i, 0))
                stage_y(At(2 * i + 1, i, 1))

            def stage_c(i, fresh=False):
                if not fresh:
                    pool.wait_ge(cm_done, i.n - 1)
                copy(cst[i.par], comb[:, bass.ds(i.n, 1), :].rearrange("p a n -> p (a n)")).then_inc(cst_ready, 1)

            pool.wait_ge(fc1_done, NPAIR)
            pool.wait_ge(yst_ready, NPAIR)
            stage_c(at(0), True)
            stage_c(at(1), True)
            with pool.Fori(1, NB // 4) as i:
                stage_c(At(2 * i, i, 0))
                stage_c(At(2 * i + 1, i, 1))

        @block.vector
        def _(dve):
            v = nc.vector

            def k_masked(b, early=False):
                dve.wait_ge(kT_ready, b.n + 1)
                if not early:
                    dve.wait_ge(sc_done, 6 * b.n - 6)
                for h in range(HEADS):
                    last = v.tensor_scalar(kM[b.par][:, h, :], kT[:, h // HPT, :],
                                           headmask[:, h % HPT:h % HPT + 1], None, ALU.mult)
                last.then_inc(kM_ready, 1)

            def v_out(b, early=False):
                dve.wait_ge(v_done, b.n + 1)
                if not early:
                    dve.wait_ge(av_done, 2 * b.n - 2)
                dst = vz[b.par].rearrange("p t (g a) f -> p (t g) a f", a=4)[:, :, 0:4:3, :]
                v.tensor_tensor(dst, ps_x[0:TP, 0:TT * D].rearrange("p (g a f) -> p g a f", a=2, f=HD),
                                bv_b.rearrange("p t (g a f) -> p (t g) a f", a=2, f=HD),
                                ALU.add).then_inc(v_ready, 1)

            def h_rows(b):
                dve.wait_ge(tr_done, b.n + 1)
                v.tensor_tensor(hb[b.par], tiles(ps_z, TP, D), bo_b, ALU.add).then_inc(hb_ready, 1)

            def prepare(b, early=False):
                k_masked(b, early)
                v_out(b, early)
                h_rows(b)

            def attention_out(b, first=False):
                dve.wait_ge(av_done, 2 * b.n + 2)
                if not first:
                    dve.wait_ge(o_done, b.n)
                v.tensor_copy(aT, tiles(ps_av, KP, NTOK)).then_inc(aT_ready, 1)

            def finish(b, early=False):
                dve.wait_ge(o_done, b.n + 1)
                dve.wait_ge(hb_ready, b.n + 1)
                if not early:
                    dve.wait_ge(kept, 3 * b.n - 3)
                v.tensor_tensor(rt[b.par], tiles(ps_y, TP, D), hb[b.par], ALU.add).then_inc(r_ready, 1)
                dve.wait_ge(r_ready, b.n + 1)
                for t in range(TT):
                    last = v.bn_stats(st[:, t, :], rt[b.par][:, t, :])
                last.then_inc(st_ready, 1)
                apart(dve, vz_zero, 1)
                dve.wait_ge(st_ready, b.n + 1)
                for t in range(TT):
                    last = v.bn_aggr(mvt[b.par][:, t, :], st[:, t, :])
                last.then_inc(mv_ready, 1)
                dve.wait_ge(mv_ready, b.n + 1)
                for t in range(TT):
                    last = v.scalar_tensor_tensor(out=ut[:, t, :], in0=rt[b.par][:, t, :],
                                                  scalar=mvt[b.par][:, t, 0:1], in1=nw_b[:, t, :],
                                                  op0=ALU.subtract, op1=ALU.mult)
                last.then_inc(u_ready, 1)
                dve.wait_ge(u_ready, b.n + 1)
                for t in range(TT):
                    last = v.tensor_tensor_reduce(out=ut[:, t, :], in0=ut[:, t, :], in1=ut[:, t, :], scale=1.0,
                                                  scalar=0.0, op0=ALU.mult, op1=ALU.add,
                                                  accum_out=sst[b.par][:, t:t + 1])
                last.then_inc(ss_ready, 1)
                dve.wait_ge(ss_ready, b.n + 1)

            dve.wait_ge(const_in, CONSTS)
            dve.wait_ge(vz_zero, 1)
            prepare(at(0), early=True)
            prepare(at(1), early=True)

            def step(b, second=False, early=False):
                attention_out(prv(b), first=second)
                finish(prv(b), early=early)
                prepare(nxt(b))

            step(at(1), second=True, early=True)
            step(at(2), early=True)
            with dve.Fori(1, NB // 2 - 1) as i:
                step(At(2 * i + 1, i, 1))
                step(At(2 * i + 2, i + 1, 0))
            attention_out(at(NB - 2))
            finish(at(NB - 2))
            attention_out(at(NB - 1))
            finish(at(NB - 1))

            made = [0]

            def table(ins):
                made[0] += 1
                ins.then_inc(tables_dve, 1)
                dve.wait_ge(tables_dve, made[0])

            def rooted(n):
                dve.wait_ge(tables_act, n)

            dve.wait_ge(kept, 3 * NB)
            table(v.tensor_scalar(tmp, mv[:, :, 1], EPS, None, ALU.add))
            table(v.tensor_tensor_reduce(out=slot_sq, in0=slot_rows, in1=slot_rows, scale=1.0, scalar=0.0,
                                         op0=ALU.mult, op1=ALU.add, accum_out=slot_s[:, 0:1]))
            rooted(1)
            table(v.reciprocal(rstd, lcoef))
            table(v.scalar_tensor_tensor(out=nmr, in0=mv[:, :, 0], scalar=-1.0, in1=rstd, op0=ALU.mult,
                                         op1=ALU.mult))
            table(v.tensor_tensor(tmp, rstd, rstd, ALU.mult))
            table(v.tensor_tensor(tmp, tmp, mv[:, :, 1], ALU.mult))
            table(v.tensor_scalar(tmp, tmp, EPS, None, ALU.add))
            rooted(3)
            table(v.reciprocal(rms, lcoef))
            rooted(4)
            table(v.tensor_tensor(tmp, ssu, rstd, ALU.mult))
            table(v.tensor_tensor(tmp, tmp, rms, ALU.mult))
            table(v.tensor_scalar(tmp, tmp, EPS, None, ALU.max))
            table(v.reciprocal(tmp, tmp))
            table(v.tensor_tensor(lcoef, tmp, rms, ALU.mult))
            table(v.tensor_scalar(slot_s[:, 1:2], slot_s[:, 1:2], EPS, None, ALU.max))
            table(v.reciprocal(slot_s[:, 2:3], slot_s[:, 1:2]))
            table(v.tensor_scalar(slot_sq, slot_rows, slot_s[:, 2:3], slot_s[:, 3:4], ALU.mult, ALU.mult))
            assert made[0] == SLOTS_AT
            dve.wait_ge(slT_done, 1)
            for k in range(KT):
                last = v.tensor_scalar(slwT[:, k, :], ps_y[0:KP, k * NS:(k + 1) * NS], nw_c[:, k:k + 1], None,
                                       ALU.mult)
            last.then_inc(slwT_ready, 1)

            def token_max(b):
                dve.wait_ge(zT_done, b.n + 1)
                v.tensor_reduce(mxt, bank(2)[0:NS, 0:NTOK], AX_X, ALU.max).then_inc(mxt_ready, 1)
                dve.wait_ge(mxt_ready, b.n + 1)
                v.tensor_scalar(nmt, mxt, -1.0, None, ALU.mult).then_inc(nmt_ready, 1)

            def over_slots(b):
                dve.wait_ge(ez_ready, b.n + 1)
                v.tensor_reduce(sm2, ez[b.par], AX_X, ALU.add).then_inc(sm_ready, 1)
                dve.wait_ge(sm_ready, b.n + 1)
                v.reciprocal(rc2, sm2).then_inc(rc_ready, 1)
                dve.wait_ge(rc_ready, b.n + 1)
                if later(b, 2):
                    dve.wait_ge(e_done, b.n - 1)
                v.tensor_tensor(en[b.par], ez[b.par], rc2.unsqueeze(2).to_broadcast([TP, TT, NS]),
                                ALU.mult).then_inc(en_ready, 1)

            def over_tokens(b):
                dve.wait_ge(pt_ready, b.n + 1)
                v.reciprocal(rzt, zt).then_inc(rzt_ready, 1)
                dve.wait_ge(rzt_ready, b.n + 1)
                if later(b, 2):
                    dve.wait_ge(d_done, b.n - 1)
                v.tensor_scalar(pn[b.par], pt[b.par], rzt, None, ALU.mult).then_inc(pn_ready, 1)

            def dispatch_rows(b):
                dve.wait_ge(d_done, b.n + 1)
                if later(b, 2):
                    dve.wait_ge(y_done, b.n - 1)
                v.tensor_tensor(dr[b.par], tiles(bank(3), TP, NS),
                                rms[:, bass.ds(2 * b.n, 2)].unsqueeze(2).to_broadcast([TP, TT, NS]),
                                ALU.mult).then_inc(dr_ready, 1)

            def logits_out(b):
                dve.wait_ge(lg_done, b.n + 1)
                if later(b, 2):
                    dve.wait_ge(zT_done, b.n - 1)
                v.tensor_tensor(zl[b.par], tiles(bank(1), TP, NS),
                                lcoef[:, bass.ds(2 * b.n, 2)].unsqueeze(2).to_broadcast([TP, TT, NS]),
                                ALU.mult).then_inc(z_ready, 1)
                dve.wait_ge(z_ready, b.n + 1)
                v.tensor_reduce(mx2, zl[b.par], AX_X, ALU.max).then_inc(mx_ready, 1)
                dve.wait_ge(mx_ready, b.n + 1)
                if later(b, 2):
                    dve.wait_ge(ez_ready, b.n - 1)
                v.tensor_tensor(zm[b.par], zl[b.par], mx2.unsqueeze(2).to_broadcast([TP, TT, NS]),
                                ALU.subtract).then_inc(zm_ready, 1)

            def dve_step(s):
                for lag, stage in ((1, logits_out), (3, dispatch_rows), (2, over_tokens), (1, over_slots),
                                   (1, token_max)):
                    if s.has(lag):
                        stage(s.back(lag))

            route(dve, dve_step)

            def hidden_out(j):
                dve.wait_ge(hidT_done, j.n + 1)
                if later(j, 1):
                    dve.wait_ge(fc2_done, j.n)
                v.tensor_copy(hidT, bank(4, 2)[:, 0:F].rearrange("p (k n) -> p k n", k=FK)
                              ).then_inc(hidT_ready, 1)

            def y2_rows(j, fresh=False):
                dve.wait_ge(fc2_done, j.n + 1)
                dve.wait_ge(b2_in[j.par], 32 * (j.half + 1))
                if not fresh:
                    dve.wait_ge(y2_out[j.par], 32 * j.half)
                v.tensor_tensor(y2o[j.par], bank(6)[:, 0:D], b2_s[j.par], ALU.add).then_inc(y2_ready, 1)

            def expert(j, fresh=False):
                hidden_out(j)
                y2_rows(j, fresh)

            expert(at(0), True)
            expert(at(1), True)
            with dve.Fori(1, NPAIR // 2) as i:
                expert(At(2 * i, i, 0))
                expert(At(2 * i + 1, i, 1))

            def pair(i, first=False, last=False, fresh=False):
                if not last:
                    dve.wait_ge(cm_done, i.n + 1)
                    if not fresh:
                        dve.wait_ge(ob_ready, i.n - 1)
                    v.tensor_tensor(rf[i.par].rearrange("p (e t) d -> p e (t d)", e=2),
                                    bank(2 * i.par, 2).rearrange("p (e n) -> p e n", e=2)[0:TP, :, 0:TT * D],
                                    res[:, bass.ds(4 * i.n, 4), :].rearrange("p (e t) d -> p e (t d)", e=2),
                                    ALU.add).then_inc(rf_ready, 1)
                if not first:
                    b = prv(i)
                    dve.wait_ge(sd4_ready, b.n + 1)
                    v.reciprocal(rs4[b.par], sd4[b.par]).then_inc(rs4_ready, 1)
                if not last:
                    dve.wait_ge(rf_ready, i.n + 1)
                    for t in range(4):
                        last_op = v.bn_stats(st4[:, t, :], rf[i.par][:, t, :])
                    last_op.then_inc(st4_ready, 1)
                if not first:
                    dve.wait_ge(rs4_ready, b.n + 1)
                    v.scalar_tensor_tensor(out=nm4[b.par], in0=mv4[b.par][:, :, 0], scalar=-1.0, in1=rs4[b.par],
                                           op0=ALU.mult, op1=ALU.mult).then_inc(nm4_ready, 1)
                if not last:
                    apart(dve, vz_zero, 1)
                    dve.wait_ge(st4_ready, i.n + 1)
                    for t in range(4):
                        last_op = v.bn_aggr(mv4[i.par][:, t, :], st4[:, t, :])
                    last_op.then_inc(mv4_ready, 1)
                    dve.wait_ge(mv4_ready, i.n + 1)
                    if not fresh:
                        dve.wait_ge(sd4_ready, i.n - 1)
                    v.tensor_scalar(ve4[i.par], mv4[i.par][:, :, 1], EPS, None, ALU.add).then_inc(ve4_ready, 1)

            dve.wait_ge(yst_ready, NPAIR)
            pair(at(0), first=True, fresh=True)
            pair(at(1), fresh=True)
            with dve.Fori(1, NB // 4) as i:
                pair(At(2 * i, i, 0))
                pair(At(2 * i + 1, i, 1))
            pair(at(NB // 2), last=True)


def kernel(**inputs):
    import numpy as np
    import concourse.bacc as bacc
    from concourse.bass_utils import run_bass_kernel_spmd

    a = {k: np.asarray(val) for k, val in inputs.items()}
    side, p = a["x"].shape[2] // 16, 16

    def rows(w, tiles):
        return w.reshape(tiles, w.shape[0] // tiles, -1).transpose(1, 0, 2)

    x = a["x"].reshape(NB, 3, side, p, side, p).transpose(0, 1, 3, 5, 2, 4)
    arrays = {
        "x": x.reshape(NB, PK, 128, NTOK).transpose(0, 2, 1, 3),
        "wp": rows(a["L0_tok_Wp"].T, PK),
        "bp": a["L0_tok_bp"].reshape(KT, KP).T,
        "attn_bias": a["L0_attn_bias"].reshape(1, 1),
        "wq": rows(a["L0_attn_Wq"].T, KT),
        "bq": a["L0_attn_bq"].reshape(KT, KP).T,
        "wk": rows(a["L0_attn_Wk"].T, KT),
        "bk": a["L0_attn_bk"].reshape(KT, KP).T,
        "wv": rows(a["L0_attn_Wv"].T, KT),
        "bv": a["L0_attn_bv"],
        "wo": rows(a["L0_attn_Wo"].T, KT),
        "bo": a["L0_attn_bo"],
        "slots": a["L0_ffn_slots"],
        "scale": a["L0_ffn_scale"].reshape(NS, 1),
        "w1": a["L0_ffn_fc1_weight"].reshape(NS, KT, KP, F).transpose(0, 2, 1, 3),
        "b1": a["L0_ffn_fc1_bias"],
        "w2": a["L0_ffn_fc2_weight"].reshape(NS, FK, 128, D).transpose(0, 2, 1, 3),
        "b2": a["L0_ffn_fc2_bias"],
        "norm_w": a["L0_ffn_norm_weight"],
        "norm_c": a["L0_ffn_norm_weight"].reshape(KT, KP).T,
        "ident": np.eye(128, dtype=np.float32),
        "mask": np.repeat(np.eye(HPT, dtype=np.float32), HD, axis=0),
    }
    nc = bacc.Bacc("TRN2", target_bir_lowering=False, num_devices=1)
    feeds, aps = {}, []
    for name, arr in arrays.items():
        arr = np.ascontiguousarray(arr)
        feeds[f"in_{name}"] = arr
        aps.append(nc.dram_tensor(f"in_{name}", arr.shape, mybir.dt.from_np(arr.dtype), kind="ExternalInput").ap())
    out = nc.dram_tensor("out", (NB, NTOK, D), F32, kind="ExternalOutput").ap()
    vit_tower(nc, *aps, out)
    r = run_bass_kernel_spmd(nc, [feeds], core_ids=[0])
    return r.results[0]["out"]
```

```python
from contextlib import ExitStack
from collections import namedtuple

import concourse.bass as bass
from concourse import mybir

F32 = mybir.dt.float32
BF16 = mybir.dt.bfloat16
ALU = mybir.AluOpType
ACT = mybir.ActivationFunctionType
AX_X = mybir.AxisListType.X

NB, NTOK, D = 64, 196, 192
PATCH = 768
HEADS, HD = 12, 16
NS, F = 64, 768
TT = 2
TP = NTOK // TT
KT = 2
KP = D // KT
PK = PATCH // 128
FK = F // 128
HPT = HEADS // KT
PAIRS = HEADS // 2
HALF = PAIRS // 2
PARTS = 3
Q_STACK, K_STACK = (0, 0, 0, 1, 1, 2), (0, 1, 2, 0, 1, 0)
STACK = len(Q_STACK) * HD
EPS = 1e-5
BANK = 512
SBUF_WORDS = 53200
NPAIR = NS // 2

At = namedtuple("At", "n half par")


def nxt(b):
    return At(b.n + 1, b.half + b.par % 2, (b.par + 1) % 2)


def prv(b):
    return At(b.n - 1, b.half - 1 + b.par % 2, (b.par + 1) % 2)


def at(n):
    return At(n, n // 2, n % 2)


def later(b, n):
    return not isinstance(b.n, int) or b.n >= n


def apart(engine, done, value):
    engine.wait_ge(done, value)


def count(engine, value):
    return value if isinstance(value, int) else engine.to_reg(value)


SLOTS_AT = 16
RING = 4
Ringed = namedtuple("Ringed", "n half par ring")


class Step:

    def __init__(self, i, u):
        self.i, self.u = i, u

    def has(self, lag):
        return not isinstance(self.i, int) or 0 <= RING * self.i + self.u - lag < NB

    def back(self, lag):
        n = self.u - lag
        return Ringed(RING * self.i + n, 2 * self.i + n // 2, n % 2, n % RING)


def route(engine, step):
    for u in range(-1, RING):
        step(Step(0, u))
    with engine.Fori(1, NB // RING - 1) as i:
        for u in range(RING):
            step(Step(i, u))
    for u in range(RING + 3):
        step(Step(NB // RING - 1, u))


class Layout:

    def __init__(self, arena, start):
        self.arena, self.at = arena, start

    def take(self, parts, *dims):
        size = 1
        for d in dims:
            size *= d
        ap = self.arena[0:parts, self.at:self.at + size]
        self.at += size
        assert self.at <= SBUF_WORDS, self.at
        names = "abcde"[:len(dims)]
        if len(dims) > 1:
            kw = {n: d for n, d in zip(names, dims)}
            ap = ap.rearrange(f"p ({' '.join(names)}) -> p {' '.join(names)}", **kw)
        return ap

    def take_bf16(self, parts, *dims):
        size = 1
        for d in dims:
            size *= d
        names = "abcde"[:len(dims)]
        kw = {n: d for n, d in zip(names, dims)}
        return self.take(parts, size // 2).bitcast(BF16).rearrange(
            f"p ({' '.join(names)}) -> p {' '.join(names)}", **kw)


def vit_tower(nc, x, wp, bp, attn_bias, wq, bq, wk, bk, wv, bv, wo, bo, slots, scale, w1, b1, w2, b2,
              norm_w, norm_c, ident_d, out):
    qk_dram = nc.dram_tensor("qk_parts", (2, 2, KP, PARTS * KT * NTOK), BF16, kind="Internal").ap()
    y2_dram = nc.dram_tensor("slot_outputs", (NB, NS, D), F32, kind="Internal").ap()

    with ExitStack() as ctx:
        def sem(name):
            return ctx.enter_context(nc.semaphore(name))

        arena = ctx.enter_context(nc.sbuf_tensor("arena", [128, SBUF_WORDS], F32))
        psum = ctx.enter_context(nc.psum_tensor("psum", [128, 8 * BANK], F32))

        def bank(i, n=1):
            return psum[:, i * BANK:(i + n) * BANK]

        keep = Layout(arena, 0)
        res = keep.take(TP, NB * TT, D)
        ident = keep.take(128, 128)
        abias = keep.take(TP, 1)
        bp_c, bq_c, bk_c, nw_c = (keep.take(KP, KT) for _ in range(4))
        slwT = keep.take(KP, KT, NS)
        tables_at = keep.at
        tab = Layout(arena, tables_at)
        mv = tab.take(TP, NB * TT, 2)
        ssu = tab.take(TP, NB * TT)
        rstd, nmr, rms, lcoef, tmp = (tab.take(TP, NB * TT) for _ in range(5))
        slot_rows = tab.take(NS, D)
        slot_sq = tab.take(NS, D)
        slot_s = tab.take(NS, 4)
        y_words, c_words, w_words = KT * NB * NS, NPAIR * NTOK, 2 * KT * F + 2 * FK * D
        big_at = SBUF_WORDS - (y_words + c_words + 2 * w_words)
        big = Layout(arena, big_at)
        comb = big.take(128, NPAIR, NTOK)
        yT = big.take(KP, KT, NB, NS)
        w_at = big.at
        w1_s, w2_s = [], []
        for _ in range(2):
            w1_s.append(big.take(KP + 1, 2, KT, F))
            w2_s.append(big.take(128, 2, FK, D))
        assert tab.at <= big_at

        p1 = Layout(arena, big_at)
        xs = [p1.take(128, PK, NTOK) for _ in range(2)]
        wp_s = p1.take(128, PK, D)
        wq_s, wk_s, wv_s, wo_s = (p1.take(KP, KT, D) for _ in range(4))
        hT = [p1.take(KP, KT, NTOK) for _ in range(2)]
        parts = [p1.take_bf16(KP, PARTS, KT, NTOK) for _ in range(2)]
        rest = [p1.take(KP, KT, NTOK) for _ in range(2)]
        stacks = [[p1.take_bf16(STACK, HPT, KT, NTOK) for _ in range(2)] for _ in range(2)]
        vz = [p1.take(TP, TT, PAIRS * 4, HD) for _ in range(2)]
        sig = p1.take(TP, PAIRS, 2, TT, NTOK)
        aT = p1.take(KP, KT, NTOK)
        hb = [p1.take(TP, TT, D) for _ in range(2)]
        bv_b, bo_b, nw_b = (p1.take(TP, TT, D) for _ in range(3))
        rt = [p1.take(TP, TT, D) for _ in range(2)]
        ut = p1.take(TP, TT, D)
        junk = p1.take(TP, D)
        st = p1.take(TP, TT, 6)
        mvt = [p1.take(TP, TT, 2) for _ in range(2)]
        sst = [p1.take(TP, TT) for _ in range(2)]

        p2 = Layout(arena, w_at + w_words)
        h1s = [p2.take(TP, TT, D) for _ in range(4)]
        hT2 = [p2.take(KP, KT, NTOK) for _ in range(2)]
        zl = [p2.take(TP, TT, NS) for _ in range(2)]
        zm = [p2.take(TP, TT, NS) for _ in range(2)]
        ez = [p2.take(TP, TT, NS) for _ in range(2)]
        en = [p2.take(TP, TT, NS) for _ in range(2)]
        pt = [p2.take(NS, NTOK) for _ in range(2)]
        pn = [p2.take(NS, NTOK) for _ in range(2)]
        dr = [p2.take(TP, TT, NS) for _ in range(2)]
        mx2, sm2, rc2 = (p2.take(TP, TT) for _ in range(3))
        mxt, nmt, zt, rzt = (p2.take(NS, 1) for _ in range(4))

        p3 = Layout(arena, tables_at)
        hid = p3.take(128, F)
        hidT = p3.take(128, FK, 128)
        yst = [p3.take(KP + 1, KT, 2, NB) for _ in range(2)]
        b2_s = [p3.take(128, D) for _ in range(2)]
        y2o = [p3.take(128, D) for _ in range(2)]
        assert p3.at <= big_at

        p4 = Layout(arena, big_at + c_words)
        y2s = [p4.take(128, D) for _ in range(2)]
        cst = [p4.take(128, NTOK) for _ in range(2)]
        rf = [p4.take(TP, 4, D) for _ in range(2)]
        ob = [p4.take(TP, 4, D) for _ in range(2)]
        st4 = p4.take(TP, 4, 6)
        mv4 = [p4.take(TP, 4, 2) for _ in range(2)]
        ve4, sd4 = ([p4.take(TP, 4) for _ in range(2)] for _ in range(2))
        rs4, nm4 = ([p4.take(TP, 4) for _ in range(2)] for _ in range(2))

        ps_sc = [bank(0, 2).rearrange("p (h n) -> p h n", h=2), bank(2, 2).rearrange("p (h n) -> p h n", h=2)]
        ps_av, ps_x, ps_y, ps_z = bank(4), bank(5), bank(6), bank(7)

        def tiles(b, p, n):
            return b[0:p, 0:2 * n].rearrange("p (t n) -> p t n", t=2)

        const_in = sem("const_in")
        x_in = [sem("x_in0"), sem("x_in1")]
        (tok_done, hT_ready, q_done, k_done, q_high, k_high, q_rest, k_rest, q_mid, k_mid, q_parts,
         k_parts, v_done, v_ready, tr_done,
         hb_ready, sc_done, sig_done, av_done, aT_ready, o_done, r_ready, st_ready, mv_ready, u_ready,
         ss_ready, kept) = (sem(n) for n in (
             "tok_done", "hT_ready", "q_done", "k_done", "q_high", "k_high", "q_rest", "k_rest", "q_mid",
             "k_mid", "q_parts", "k_parts", "v_done",
             "v_ready", "tr_done", "hb_ready", "sc_done", "sig_done", "av_done", "aT_ready", "o_done",
             "r_ready", "st_ready", "mv_ready", "u_ready", "ss_ready", "kept"))
        vz_zero = sem("vz_zero")
        parts_out = [sem("q_parts_out"), sem("k_parts_out")]
        stack_in = [sem("stack_in0"), sem("stack_in1")]
        tables_dve, tables_act, slT_done, slwT_ready = (sem(n) for n in (
            "tables_dve", "tables_act", "slT_done", "slwT_ready"))
        (h1_ready, h1_kept, hT2_done, hT2_ready, lg_done, z_ready, mx_ready, zm_ready, ez_ready, sm_ready,
         rc_ready, en_ready, zT_done, mxt_ready, nmt_ready, pt_ready, rzt_ready, pn_ready, d_done,
         dr_ready, e_done, comb_ready, y_done, yT_ready) = (sem(n) for n in (
             "h1_ready", "h1_kept", "hT2_done", "hT2_ready", "lg_done", "z_ready", "mx_ready", "zm_ready",
             "ez_ready", "sm_ready", "rc_ready", "en_ready", "zT_done", "mxt_ready", "nmt_ready",
             "pt_ready", "rzt_ready", "pn_ready", "d_done", "dr_ready", "e_done", "comb_ready", "y_done",
             "yT_ready"))
        w1_in = [sem("w1_in0"), sem("w1_in1")]
        w2_in = [sem("w2_in0"), sem("w2_in1")]
        b2_in = [sem("b2_in0"), sem("b2_in1")]
        (yst_ready, ones_set, fc1_done, hid_ready, hidT_done, hidT_ready, fc2_done, y2_ready) = (
            sem(n) for n in ("yst_ready", "ones_set", "fc1_done", "hid_ready", "hidT_done", "hidT_ready",
                             "fc2_done", "y2_ready"))
        y2_out = [sem("y2_out0"), sem("y2_out1")]
        y2_in = [sem("y2_in0"), sem("y2_in1")]
        (cst_ready, cm_done, rf_ready, st4_ready, mv4_ready, ve4_ready, sd4_ready, rs4_ready,
         nm4_ready, ob_ready) = (sem(n) for n in ("cst_ready", "cm_done", "rf_ready", "st4_ready", "mv4_ready",
                                       "ve4_ready", "sd4_ready", "rs4_ready", "nm4_ready",
                                       "ob_ready"))
        out_done = [sem("out_done0"), sem("out_done1")]

        consts = [
            (wp_s, wp), (bp_c, bp), (wq_s, wq), (bq_c, bq), (wk_s, wk), (bk_c, bk),
            (wv_s, wv), (wo_s, wo), (ident, ident_d), (nw_c, norm_c),
            (abias, attn_bias.to_broadcast([TP, 1])),
            (slot_rows, slots), (slot_s[:, 3:4], scale),
        ]
        for tile, row in ((bv_b, bv), (bo_b, bo), (nw_b, norm_w)):
            for t in range(TT):
                consts.append((tile[:, t, :], row.rearrange("(a d) -> a d", a=1).to_broadcast([TP, D])))
        CONSTS = 16 * len(consts)

        out_v = out.rearrange("b (t p) d -> p (b t) d", p=TP)
        block = ctx.enter_context(nc.Block())

        @block.sync
        def _(sp):
            def load_x(b):
                sp.wait_ge(tok_done, b.n - 1)
                sp.dma_start(xs[b.par], x[bass.ds(b.n, 1)].rearrange("a p k n -> (a p) k n")
                             ).then_inc(x_in[b.par], 16)

            def restack(b, fresh=False):
                for w, made in ((0, q_parts), (1, k_parts)):
                    if w == 0 and not fresh:
                        sp.wait_ge(stack_in[b.par], 16 * 2 * len(Q_STACK) * b.half)
                    sp.wait_ge(made, b.n + 1)
                    sp.dma_start(qk_dram[b.par, w], parts[w].rearrange("p c k n -> p (c k n)")
                                 ).then_inc(parts_out[w], 16)
                if not fresh:
                    sp.wait_ge(sc_done, PAIRS * (b.n - 1))
                for w, order in ((0, Q_STACK), (1, K_STACK)):
                    sp.wait_ge(parts_out[w], 16 * b.n + 16)
                    src = qk_dram[b.par, w].rearrange("(h f) (c n) -> c f h n", f=HD, c=PARTS)
                    for i, part in enumerate(order):
                        sp.dma_start(stacks[w][b.par][HD * i:HD * (i + 1)].rearrange("p h k n -> p h (k n)"),
                                     src[part]).then_inc(stack_in[b.par], 16)

            for n in range(2):
                sp.dma_start(xs[n], x[n]).then_inc(x_in[n], 16)
                for tile, src in (consts[0:6] if n == 0 else consts[6:]):
                    sp.dma_start(tile, src).then_inc(const_in, 16)
            def step(b, more=True, fresh=False):
                if more:
                    load_x(nxt(nxt(b)))
                restack(b, fresh)

            step(at(0), fresh=True)
            step(at(1), fresh=True)
            with sp.Fori(1, NB // 2 - 1) as i:
                step(At(2 * i, i, 0))
                step(At(2 * i + 1, i, 1))
            step(at(NB - 2), more=False)
            step(at(NB - 1), more=False)

            def load_w1(j):
                if later(j, 2):
                    sp.wait_ge(fc1_done, j.n - 1)
                w1_t = w1_s[j.par]
                sp.dma_start(w1_t[0:KP].rearrange("p s k f -> p s (k f)"),
                             w1[bass.ds(2 * j.n, 2)].rearrange("s p k f -> p s (k f)")).then_inc(w1_in[j.par], 16)
                sp.dma_start(w1_t[KP:KP + 1, :, KT - 1, :],
                             b1[bass.ds(2 * j.n, 2)].rearrange("(a s) f -> a s f", a=1)).then_inc(w1_in[j.par], 16)

            def load_w2(j):
                if later(j, 2):
                    sp.wait_ge(fc2_done, j.n - 1)
                sp.dma_start(w2_s[j.par].rearrange("p s k d -> p s (k d)"),
                             w2[bass.ds(2 * j.n, 2)].rearrange("s p k d -> p s (k d)")).then_inc(w2_in[j.par], 16)

            def load_b2(j):
                if later(j, 2):
                    sp.wait_ge(y2_ready, j.n - 1)
                for s in range(2):
                    sp.dma_start(b2_s[j.par][64 * s:64 * s + 64, :],
                                 b2[bass.ds(2 * j.n + s, 1), :].to_broadcast([NB, D])).then_inc(b2_in[j.par], 16)

            def store_y2(j):
                sp.wait_ge(y2_ready, j.n + 1)
                for s in range(2):
                    sp.dma_start(y2_dram[:, bass.ds(2 * j.n + s, 1), :].rearrange("b a d -> (b a) d"),
                                 y2o[j.par][64 * s:64 * s + 64, :]).then_inc(y2_out[j.par], 16)

            sp.wait_ge(kept, 3 * NB)
            load_w1(at(0))
            load_w2(at(0))
            sp.wait_ge(yT_ready, NB)
            sp.wait_ge(comb_ready, NB)
            sp.wait_ge(h1_kept, NB)
            load_b2(at(0))
            load_w1(at(1))
            load_w2(at(1))
            load_b2(at(1))
            with sp.Fori(0, NPAIR // 2 - 1) as i:
                for u in range(2):
                    j = At(2 * i + u, i, u)
                    load_w1(At(2 * i + u + 2, i + 1, u))
                    load_w2(At(2 * i + u + 2, i + 1, u))
                    load_b2(At(2 * i + u + 2, i + 1, u))
                    store_y2(j)
            for n in (NPAIR - 2, NPAIR - 1):
                store_y2(at(n))

            for s in y2_out:
                sp.wait_ge(s, 32 * (NPAIR // 2))

            def load_y2(i):
                sp.dma_start(y2s[i.par], y2_dram[bass.ds(2 * i.n, 2)].rearrange("b s d -> (b s) d")
                             ).then_inc(y2_in[i.par], 16)

            load_y2(at(0))
            load_y2(at(1))
            with sp.Fori(0, NB // 4 - 1) as i:
                for u in range(2):
                    sp.wait_ge(cm_done, 2 * i + u + 1)
                    load_y2(At(2 * i + u + 2, i + 1, u))
            for s in out_done:
                sp.wait_ge(s, 16 * (NB // 4))

        @block.tensor
        def _(pe):
            mm, tr = nc.tensor.matmul, nc.tensor.transpose

            def tok(b, m):
                if m == 0:
                    pe.wait_ge(x_in[b.par], 16 * (b.half + 1))
                    if later(b, 2):
                        pe.wait_ge(v_ready, b.n - 1)
                    elif b.n == 1:
                        pe.wait_ge(hT_ready, 1)
                o = tiles(ps_x, KP, NTOK)
                for k in range(PK):
                    last = mm(o[:, m, :], wp_s[:, k, m * KP:(m + 1) * KP], xs[b.par][:, k, :],
                              start=k == 0, stop=k == PK - 1)
                if m == KT - 1:
                    last.then_inc(tok_done, 1)

            def project(b, w, bankap, done):
                o = tiles(bankap, KP, NTOK)
                for m in range(KT):
                    for k in range(KT):
                        last = mm(o[:, m, :], w[:, k, m * KP:(m + 1) * KP], hT[b.par][:, k, :],
                                  start=k == 0, stop=k == KT - 1)
                last.then_inc(done, 1)

            def q_proj(b):
                pe.wait_ge(hT_ready, b.n + 1)
                if later(b, 3):
                    pe.wait_ge(r_ready, b.n - 2)
                elif b.n == 1:
                    pe.wait_ge(q_rest, 1)
                project(b, wq_s, ps_y, q_done)

            def k_proj(b):
                if later(b, 2):
                    pe.wait_ge(hb_ready, b.n - 1)
                elif b.n == 1:
                    pe.wait_ge(k_rest, 1)
                project(b, wk_s, ps_z, k_done)

            def by_token(lhs, w, bankap, done):
                o = tiles(bankap, TP, D)
                for t in range(TT):
                    for k in range(KT):
                        last = mm(o[:, t, :], lhs[:, k, t * TP:(t + 1) * TP], w[:, k, :],
                                  start=k == 0, stop=k == KT - 1)
                last.then_inc(done, 1)

            def v_h(b, last_one=False):
                ahead = b.n + (1 if last_one else 2)
                pe.wait_ge(hT_ready, ahead)
                by_token(hT[b.par], wv_s, ps_x, v_done)
                pe.wait_ge(k_rest, ahead)
                o = tiles(ps_z, TP, D)
                for t in range(TT):
                    for k in range(KT):
                        last = tr(o[:, t, k * KP:(k + 1) * KP], hT[b.par][:, k, t * TP:(t + 1) * TP],
                                  ident[0:KP, 0:KP])
                last.then_inc(tr_done, 1)

            def scores(b, g, first=False):
                if g == 0:
                    pe.wait_ge(stack_in[b.par], 16 * 2 * len(Q_STACK) * (b.half + 1))
                if not (first and g < 2):
                    pe.wait_ge(sig_done, 6 * b.n + g - 1)
                q_st, k_st = stacks[0][b.par], stacks[1][b.par]
                for a in range(2):
                    h = 2 * g + a
                    for t in range(TT):
                        last = mm(ps_sc[g % 2][0:TP, a, t * NTOK:(t + 1) * NTOK],
                                  k_st[:, h % HPT, h // HPT, t * TP:(t + 1) * TP], q_st[:, h % HPT, h // HPT, :],
                                  start=True, stop=True)
                last.then_inc(sc_done, 1)

            def attend(b, half, first=False):
                pe.wait_ge(sig_done, 6 * b.n + 3 * half + 3)
                if half == 0:
                    pe.wait_ge(v_ready, b.n + 1)
                    if not first:
                        pe.wait_ge(aT_ready, b.n)
                for a in range(2):
                    for t in range(TT):
                        for c in range(HALF):
                            g = HALF * half + c
                            vt = vz[b.par][:, t, 4 * g + 2 * a:4 * g + 2 * a + 2, :]
                            last = mm(ps_av[32 * c:32 * c + 32, half * NTOK:(half + 1) * NTOK],
                                      vt.rearrange("p a f -> p (a f)"), sig[:, g, a, t, :],
                                      start=a == 0 and t == 0, stop=a == 1 and t == TT - 1)
                last.then_inc(av_done, 1)

            def o_proj(b):
                pe.wait_ge(aT_ready, b.n + 1)
                pe.wait_ge(q_rest, min(b.n + 3, NB) if isinstance(b.n, int) else b.n + 3)
                by_token(aT, wo_s, ps_y, o_done)

            def step(b, first=False, project_next=True, value_next=True):
                ahead = nxt(nxt(b))
                scores(b, 0, first)
                if not first:
                    attend(prv(b), 1)
                scores(b, 1, first)
                if project_next:
                    tok(ahead, 0)
                scores(b, 2)
                if project_next:
                    tok(ahead, 1)
                scores(b, 3)
                if not first:
                    o_proj(prv(b))
                scores(b, 4)
                if project_next:
                    q_proj(ahead)
                attend(b, 0, first)
                scores(b, 5)
                if project_next:
                    k_proj(ahead)
                if value_next:
                    v_h(nxt(b), last_one=not project_next)

            pe.wait_ge(const_in, CONSTS)
            for n in range(2):
                for m in range(KT):
                    tok(at(n), m)
                q_proj(at(n))
                k_proj(at(n))
            v_h(at(0))
            step(at(0), first=True)
            with pe.Fori(0, NB // 2 - 2) as i:
                step(At(2 * i + 1, i, 1))
                step(At(2 * i + 2, i + 1, 0))
            step(at(NB - 3))
            step(at(NB - 2), project_next=False)
            step(at(NB - 1), project_next=False, value_next=False)
            attend(at(NB - 1), 1)
            o_proj(at(NB - 1))

            pe.wait_ge(tables_dve, SLOTS_AT)
            pe.wait_ge(r_ready, NB)
            for k in range(KT):
                last = tr(ps_y[0:KP, k * NS:(k + 1) * NS], slot_sq[:, k * KP:(k + 1) * KP], ident[0:NS, 0:NS])
            last.then_inc(slT_done, 1)
            pe.wait_ge(slwT_ready, 1)

            def h_transposed(b):
                pe.wait_ge(h1_ready, b.n + 1)
                if later(b, 1):
                    pe.wait_ge(hT2_ready, b.n)
                o = tiles(bank(0), KP, NTOK)
                for k in range(KT):
                    for t in range(TT):
                        last = tr(o[:, k, t * TP:(t + 1) * TP], h1s[b.ring][:, t, k * KP:(k + 1) * KP],
                                  ident[0:TP, 0:TP])
                last.then_inc(hT2_done, 1)

            def logits(b):
                pe.wait_ge(hT2_ready, b.n + 1)
                if later(b, 1):
                    pe.wait_ge(z_ready, b.n)
                o = tiles(bank(1), TP, NS)
                for t in range(TT):
                    for k in range(KT):
                        last = mm(o[:, t, :], hT2[b.par][:, k, t * TP:(t + 1) * TP], slwT[:, k, :],
                                  start=k == 0, stop=k == KT - 1)
                last.then_inc(lg_done, 1)

            def z_waits(b):
                pe.wait_ge(z_ready, b.n + 1)
                if later(b, 1):
                    pe.wait_ge(pt_ready, b.n)

            def weight_waits(b):
                pe.wait_ge(pn_ready, b.n + 1)
                pe.wait_ge(en_ready, b.n + 1)
                if later(b, 1):
                    pe.wait_ge(dr_ready, b.n)
                    pe.wait_ge(comb_ready, b.n)

            def z_transposed(b):
                for t in range(TT):
                    last = tr(bank(2)[0:NS, t * TP:(t + 1) * TP], zl[b.par][:, t, :], ident[0:TP, 0:TP])
                last.then_inc(zT_done, 1)

            def weights_transposed(b):
                for t in range(TT):
                    last = tr(bank(3)[0:TP, t * NS:(t + 1) * NS], pn[b.par][:, t * TP:(t + 1) * TP],
                              ident[0:NS, 0:NS])
                last.then_inc(d_done, 1)
                for t in range(TT):
                    last = tr(bank(4)[0:NS, t * TP:(t + 1) * TP], en[b.par][:, t, :], ident[0:TP, 0:TP])
                last.then_inc(e_done, 1)

            def slot_inputs(b):
                pe.wait_ge(dr_ready, b.n + 1)
                if later(b, 1):
                    pe.wait_ge(yT_ready, b.n)
                o = tiles(bank(5), KP, NS)
                for k in range(KT):
                    for t in range(TT):
                        last = mm(o[:, k, :], h1s[b.ring][:, t, k * KP:(k + 1) * KP], dr[b.par][:, t, :],
                                  start=t == 0, stop=t == TT - 1)
                last.then_inc(y_done, 1)

            def pe_step(s):
                for lag, stage in ((3, weight_waits), (1, logits), (3, weights_transposed), (0, h_transposed),
                                   (1, z_waits), (3, slot_inputs), (1, z_transposed)):
                    if s.has(lag):
                        stage(s.back(lag))

            route(pe, pe_step)

            pe.wait_ge(yT_ready, NB)
            pe.wait_ge(comb_ready, NB)
            pe.wait_ge(ones_set, 2)

            def fc1(j, fresh=False):
                pe.wait_ge(w1_in[j.par], 32 * (j.half + 1))
                pe.wait_ge(yst_ready, j.n + 1)
                if not fresh:
                    pe.wait_ge(hid_ready, j.n - 1)
                for half in range(2):
                    for k in range(KT):
                        K = KP + 1 if k == KT - 1 else KP
                        for s in range(2):
                            last = mm(bank(2 * j.par + half)[64 * s:64 * s + 64, 0:F // 2],
                                      yst[j.par][0:K, k, s, :],
                                      w1_s[j.par][0:K, s, k, half * (F // 2):(half + 1) * (F // 2)],
                                      start=k == 0, stop=k == KT - 1)
                last.then_inc(fc1_done, 1)

            def hidden_transposed(j):
                pe.wait_ge(hid_ready, j.n + 1)
                if later(j, 1):
                    pe.wait_ge(hidT_ready, j.n)
                for k in range(FK):
                    last = tr(bank(4, 2)[:, k * 128:(k + 1) * 128], hid[:, k * 128:(k + 1) * 128], ident)
                last.then_inc(hidT_done, 1)

            def fc2(j):
                pe.wait_ge(w2_in[j.par], 16 * (j.half + 1))
                pe.wait_ge(hidT_ready, j.n + 1)
                if later(j, 1):
                    pe.wait_ge(y2_ready, j.n)
                for k in range(FK):
                    for s in range(2):
                        last = mm(bank(6)[64 * s:64 * s + 64, 0:D], hidT[:, k, 64 * s:64 * s + 64],
                                  w2_s[j.par][:, s, k, :], start=k == 0, stop=k == FK - 1)
                last.then_inc(fc2_done, 1)

            def expert(j, last=False, fresh=False):
                hidden_transposed(j)
                if not last:
                    fc1(nxt(j), fresh)
                fc2(j)

            fc1(at(0), fresh=True)
            expert(at(0), fresh=True)
            with pe.Fori(0, NPAIR // 2 - 1) as i:
                expert(At(2 * i + 1, i, 1))
                expert(At(2 * i + 2, i + 1, 0))
            expert(at(NPAIR - 1), last=True)

            def combine(i, fresh=False):
                pe.wait_ge(y2_in[i.par], 16 * (i.half + 1))
                pe.wait_ge(cst_ready, i.n + 1)
                if not fresh:
                    pe.wait_ge(rf_ready, i.n - 1)
                for t in range(TT):
                    for e in range(2):
                        last = mm(bank(2 * i.par + e)[0:TP, t * D:(t + 1) * D],
                                  cst[i.par][64 * e:64 * e + 64, t * TP:(t + 1) * TP],
                                  y2s[i.par][64 * e:64 * e + 64, :], start=True, stop=True)
                last.then_inc(cm_done, 1)

            pe.wait_ge(hid_ready, NPAIR)
            combine(at(0), fresh=True)
            combine(at(1), fresh=True)
            with pe.Fori(1, NB // 4) as i:
                combine(At(2 * i, i, 0))
                combine(At(2 * i + 1, i, 1))

        @block.scalar
        def _(act):
            fn = nc.scalar.activation

            def sigmoid(b, g, first=False):
                act.wait_ge(sc_done, 6 * b.n + g + 1)
                if not first:
                    act.wait_ge(av_done, 2 * b.n + g // HALF - 1)
                fn(sig[:, g].rearrange("p a t n -> p a (t n)"), ps_sc[g % 2][0:TP, :, 0:TT * NTOK],
                   ACT.Sigmoid, bias=abias, scale=float(D) ** -0.5).then_inc(sig_done, 1)

            def biased(dst, bankap, bias, ready):
                src = tiles(bankap, KP, NTOK)
                for m in range(KT):
                    last = fn(dst[:, m, :], src[:, m, :], ACT.Identity, bias=bias[:, m:m + 1])
                last.then_inc(ready, 1)

            def h_out(b):
                act.wait_ge(tok_done, b.n + 1)
                if later(b, 2):
                    act.wait_ge(tr_done, b.n - 1)
                biased(hT[b.par], ps_x, bp_c, hT_ready)

            def high_part(b, w):
                act.wait_ge((q_done, k_done)[w], b.n + 1)
                if later(b, 1):
                    act.wait_ge(parts_out[w], 16 * b.n)
                biased(parts[w][:, 0], (ps_y, ps_z)[w], (bq_c, bk_c)[w], (q_high, k_high)[w])

            def step(b, first=False, project_next=True):
                ahead = nxt(nxt(b))
                for g in range(4):
                    sigmoid(b, g, first)
                if project_next:
                    h_out(ahead)
                sigmoid(b, 4, first)
                if project_next:
                    high_part(ahead, 0)
                sigmoid(b, 5, first)
                if project_next:
                    high_part(ahead, 1)

            act.wait_ge(const_in, CONSTS)
            for n in range(2):
                h_out(at(n))
                high_part(at(n), 0)
                high_part(at(n), 1)
            step(at(0), first=True)
            with act.Fori(0, NB // 2 - 2) as i:
                step(At(2 * i + 1, i, 1))
                step(At(2 * i + 2, i + 1, 0))
            step(at(NB - 3))
            step(at(NB - 2), project_next=False)
            step(at(NB - 1), project_next=False)

            act.wait_ge(tables_dve, 1)
            fn(lcoef, tmp, ACT.Sqrt).then_inc(tables_act, 1)
            act.wait_ge(tables_dve, 2)
            fn(slot_s[:, 1:2], slot_s[:, 0:1], ACT.Sqrt).then_inc(tables_act, 1)
            act.wait_ge(tables_dve, 7)
            fn(lcoef, tmp, ACT.Sqrt).then_inc(tables_act, 1)
            fn(ssu, ssu, ACT.Sqrt).then_inc(tables_act, 1)

            def normalise(b):
                if later(b, 4):
                    act.wait_ge(y_done, b.n - 3)
                    act.wait_ge(h1_kept, b.n - 3)
                for t in range(TT):
                    row = bass.ds(2 * b.n + t, 1)
                    last = fn(h1s[b.ring][:, t, :], res[:, row, :].rearrange("p a d -> p (a d)"), ACT.Identity,
                              bias=nmr[:, row], scale=rstd[:, row])
                last.then_inc(h1_ready, 1)

            def hT2_out(b):
                act.wait_ge(hT2_done, b.n + 1)
                if later(b, 2):
                    act.wait_ge(lg_done, b.n - 1)
                fn(hT2[b.par], tiles(bank(0), KP, NTOK), ACT.Identity).then_inc(hT2_ready, 1)

            def exp_slots(b):
                act.wait_ge(zm_ready, b.n + 1)
                if later(b, 2):
                    act.wait_ge(en_ready, b.n - 1)
                fn(ez[b.par], zm[b.par], ACT.Exp).then_inc(ez_ready, 1)

            def exp_tokens(b):
                act.wait_ge(zT_done, b.n + 1)
                act.wait_ge(nmt_ready, b.n + 1)
                if later(b, 1):
                    act.wait_ge(pn_ready, b.n)
                fn(pt[b.par], bank(2)[0:NS, 0:NTOK], ACT.Exp, bias=nmt, accum_out=zt).then_inc(pt_ready, 1)

            def comb_out(b):
                act.wait_ge(e_done, b.n + 1)
                fn(comb[64 * b.par:64 * b.par + 64, bass.ds(b.half, 1), :].rearrange("p a n -> p (a n)"),
                   bank(4)[0:NS, 0:NTOK], ACT.Copy).then_inc(comb_ready, 1)

            def yT_out(b):
                act.wait_ge(y_done, b.n + 1)
                for k in range(KT):
                    last = fn(yT[:, k, bass.ds(b.n, 1), :].rearrange("p a s -> p (a s)"),
                              bank(5)[0:KP, k * NS:(k + 1) * NS], ACT.Copy, scale=nw_c[:, k:k + 1])
                last.then_inc(yT_ready, 1)

            def act_step(s):
                for lag, stage in ((2, exp_tokens), (0, hT2_out), (1, exp_slots), (3, comb_out),
                                   (3, yT_out), (-1, normalise)):
                    if s.has(lag):
                        stage(s.back(lag))

            act.wait_ge(slwT_ready, 1)
            route(act, act_step)

            def gelu(j):
                act.wait_ge(fc1_done, j.n + 1)
                if later(j, 1):
                    act.wait_ge(hidT_done, j.n)
                fn(hid.rearrange("p (h f) -> p h f", h=2),
                   bank(2 * j.par, 2).rearrange("p (h f) -> p h f", h=2)[:, :, 0:F // 2],
                   ACT.Gelu).then_inc(hid_ready, 1)

            gelu(at(0))
            with act.Fori(0, NPAIR // 2 - 1) as i:
                gelu(At(2 * i + 1, i, 1))
                gelu(At(2 * i + 2, i + 1, 0))
            gelu(at(NPAIR - 1))

            def root(i, fresh=False):
                act.wait_ge(ve4_ready, i.n + 1)
                if not fresh:
                    act.wait_ge(rs4_ready, i.n - 1)
                fn(sd4[i.par], ve4[i.par], ACT.Sqrt).then_inc(sd4_ready, 1)

            def final(i, fresh=False):
                act.wait_ge(nm4_ready, i.n + 1)
                if not fresh:
                    act.wait_ge(out_done[i.par], 16 * i.half)
                for t in range(4):
                    last = fn(ob[i.par][:, t, :], rf[i.par][:, t, :], ACT.Identity, bias=nm4[i.par][:, t:t + 1],
                              scale=rs4[i.par][:, t:t + 1])
                last.then_inc(ob_ready, 1)
                act.wait_ge(ob_ready, i.n + 1)
                act.dma_start(out_v[:, bass.ds(4 * i.n, 4), :], ob[i.par]).then_inc(out_done[i.par], 16)

            root(at(0), True)
            root(at(1), True)
            final(at(0), True)
            root(at(2))
            final(at(1), True)
            with act.Fori(1, NB // 4 - 1) as i:
                root(At(2 * i + 1, i, 1))
                final(At(2 * i, i, 0))
                root(At(2 * i + 2, i + 1, 0))
                final(At(2 * i + 1, i, 1))
            root(at(NB // 2 - 1))
            final(at(NB // 2 - 2))
            final(at(NB // 2 - 1))

        @block.gpsimd
        def _(pool):
            copy = nc.gpsimd.tensor_copy
            for v in vz:
                last = nc.gpsimd.memset(v, 0.0)
            last.then_inc(vz_zero, 1)

            def keep_rows(b):
                pool.wait_ge(r_ready, b.n + 1)
                copy(res[:, bass.ds(2 * b.n, 2), :], rt[b.par]).then_inc(kept, 1)
                pool.wait_ge(mv_ready, b.n + 1)
                copy(mv[:, bass.ds(2 * b.n, 2), :], mvt[b.par]).then_inc(kept, 1)
                pool.wait_ge(ss_ready, b.n + 1)
                copy(ssu[:, bass.ds(2 * b.n, 2)], sst[b.par]).then_inc(kept, 1)

            def middle_part(b):
                made_n = count(pool, b.n + 1)
                for w, (rests, mid) in enumerate(((q_rest, q_mid), (k_rest, k_mid))):
                    apart(pool, const_in, CONSTS)
                    pool.wait_ge(rests, made_n)
                    copy(parts[w][:, 1], rest[w]).then_inc(mid, 1)

            for n in range(2):
                middle_part(at(n))
            middle_part(at(2))
            with pool.Fori(1, NB // 2 - 1) as i:
                for b in (At(2 * i, i, 0), At(2 * i + 1, i, 1)):
                    keep_rows(prv(prv(b)))
                    middle_part(nxt(b))
            for b in (at(NB - 2), at(NB - 1)):
                keep_rows(prv(prv(b)))
                if b.n < NB - 1:
                    middle_part(nxt(b))
            keep_rows(at(NB - 2))
            keep_rows(at(NB - 1))

            with pool.Fori(0, NB // 4) as i:
                for u in range(4):
                    pool.wait_ge(h1_ready, 4 * i + u + 1)
                    copy(res[:, bass.ds(8 * i + 2 * u, 2), :], h1s[u]).then_inc(h1_kept, 1)

            pool.wait_ge(yT_ready, NB)
            pool.wait_ge(comb_ready, NB)
            pool.wait_ge(h1_kept, NB)
            for n, y in enumerate(yst):
                nc.gpsimd.memset(y[KP:KP + 1], 1.0).then_inc(ones_set, 1)
                pool.wait_ge(ones_set, n + 1)

            def stage_y(j, fresh=False):
                if not fresh:
                    pool.wait_ge(fc1_done, j.n - 1)
                for k in range(KT):
                    last = copy(yst[j.par][0:KP, k], yT[:, k, :, bass.ds(2 * j.n, 2)].rearrange("p b s -> p s b"))
                last.then_inc(yst_ready, 1)

            stage_y(at(0), True)
            stage_y(at(1), True)
            with pool.Fori(1, NPAIR // 2) as i:
                stage_y(At(2 * i, i, 0))
                stage_y(At(2 * i + 1, i, 1))

            def stage_c(i, fresh=False):
                if not fresh:
                    pool.wait_ge(cm_done, i.n - 1)
                copy(cst[i.par], comb[:, bass.ds(i.n, 1), :].rearrange("p a n -> p (a n)")).then_inc(cst_ready, 1)

            pool.wait_ge(fc1_done, NPAIR)
            pool.wait_ge(yst_ready, NPAIR)
            stage_c(at(0), True)
            stage_c(at(1), True)
            with pool.Fori(1, NB // 4) as i:
                stage_c(At(2 * i, i, 0))
                stage_c(At(2 * i + 1, i, 1))

        @block.vector
        def _(dve):
            v = nc.vector

            def rests(b, w):
                done, ready = (q_high, k_high)[w], (q_rest, k_rest)[w]
                dve.wait_ge(done, b.n + 1)
                if later(b, 1):
                    dve.wait_ge((q_parts, k_parts)[w], b.n)
                src = tiles((ps_y, ps_z)[w], KP, NTOK)
                for m in range(KT):
                    last = v.scalar_tensor_tensor(out=rest[w][:, m, :], in0=src[:, m, :],
                                                  scalar=(bq_c, bk_c)[w][:, m:m + 1], in1=parts[w][:, 0, m, :],
                                                  op0=ALU.add, op1=ALU.subtract)
                last.then_inc(ready, 1)

            def low_part(b, w):
                dve.wait_ge((q_mid, k_mid)[w], b.n + 1)
                v.tensor_tensor(parts[w][:, 2], rest[w], parts[w][:, 1], ALU.subtract
                                ).then_inc((q_parts, k_parts)[w], 1)

            def v_out(b):
                dve.wait_ge(v_done, b.n + 1)
                if later(b, 2):
                    dve.wait_ge(av_done, 2 * b.n - 2)
                dst = vz[b.par].rearrange("p t (g a) f -> p (t g) a f", a=4)[:, :, 0:4:3, :]
                v.tensor_tensor(dst, ps_x[0:TP, 0:TT * D].rearrange("p (g a f) -> p g a f", a=2, f=HD),
                                bv_b.rearrange("p t (g a f) -> p (t g) a f", a=2, f=HD),
                                ALU.add).then_inc(v_ready, 1)

            def h_rows(b):
                dve.wait_ge(tr_done, b.n + 1)
                v.tensor_tensor(hb[b.par], tiles(ps_z, TP, D), bo_b, ALU.add).then_inc(hb_ready, 1)

            def attention_out(b, first=False):
                dve.wait_ge(av_done, 2 * b.n + 2)
                if not first:
                    dve.wait_ge(o_done, b.n)
                v.tensor_copy(aT, tiles(ps_av, KP, NTOK)).then_inc(aT_ready, 1)

            def finish(b, early=False):
                dve.wait_ge(o_done, b.n + 1)
                dve.wait_ge(hb_ready, b.n + 1)
                if not early:
                    dve.wait_ge(kept, 3 * b.n - 3)
                v.tensor_tensor(rt[b.par], tiles(ps_y, TP, D), hb[b.par], ALU.add).then_inc(r_ready, 1)
                dve.wait_ge(r_ready, b.n + 1)
                for t in range(TT):
                    last = v.bn_stats(st[:, t, :], rt[b.par][:, t, :])
                last.then_inc(st_ready, 1)
                apart(dve, vz_zero, 1)
                dve.wait_ge(st_ready, b.n + 1)
                for t in range(TT):
                    last = v.bn_aggr(mvt[b.par][:, t, :], st[:, t, :])
                last.then_inc(mv_ready, 1)
                dve.wait_ge(mv_ready, b.n + 1)
                for t in range(TT):
                    last = v.scalar_tensor_tensor(out=ut[:, t, :], in0=rt[b.par][:, t, :],
                                                  scalar=mvt[b.par][:, t, 0:1], in1=nw_b[:, t, :],
                                                  op0=ALU.subtract, op1=ALU.mult)
                last.then_inc(u_ready, 1)
                dve.wait_ge(u_ready, b.n + 1)
                for t in range(TT):
                    last = v.tensor_tensor_reduce(out=ut[:, t, :], in0=ut[:, t, :], in1=ut[:, t, :], scale=1.0,
                                                  scalar=0.0, op0=ALU.mult, op1=ALU.add,
                                                  accum_out=sst[b.par][:, t:t + 1])
                last.then_inc(ss_ready, 1)
                dve.wait_ge(ss_ready, b.n + 1)

            def step(b, first=False, early=False, project_next=True, value_next=True):
                if not first:
                    attention_out(prv(b), first=early and b.n == 1)
                    finish(prv(b), early=early)
                ahead = nxt(nxt(b))
                if project_next:
                    rests(ahead, 0)
                    rests(ahead, 1)
                    low_part(ahead, 0)
                if value_next:
                    v_out(nxt(b))
                    h_rows(nxt(b))
                if project_next:
                    low_part(ahead, 1)

            dve.wait_ge(const_in, CONSTS)
            dve.wait_ge(vz_zero, 1)
            for n in range(2):
                rests(at(n), 0)
                rests(at(n), 1)
                low_part(at(n), 0)
                low_part(at(n), 1)
            v_out(at(0))
            h_rows(at(0))
            step(at(0), first=True)
            step(at(1), early=True)
            step(at(2), early=True)
            with dve.Fori(1, NB // 2 - 2) as i:
                step(At(2 * i + 1, i, 1))
                step(At(2 * i + 2, i + 1, 0))
            step(at(NB - 3))
            step(at(NB - 2), project_next=False)
            step(at(NB - 1), project_next=False, value_next=False)
            attention_out(at(NB - 1))
            finish(at(NB - 1))

            made = [0]

            def table(ins):
                made[0] += 1
                ins.then_inc(tables_dve, 1)
                dve.wait_ge(tables_dve, made[0])

            def rooted(n):
                dve.wait_ge(tables_act, n)

            dve.wait_ge(kept, 3 * NB)
            table(v.tensor_scalar(tmp, mv[:, :, 1], EPS, None, ALU.add))
            table(v.tensor_tensor_reduce(out=slot_sq, in0=slot_rows, in1=slot_rows, scale=1.0, scalar=0.0,
                                         op0=ALU.mult, op1=ALU.add, accum_out=slot_s[:, 0:1]))
            rooted(1)
            table(v.reciprocal(rstd, lcoef))
            table(v.scalar_tensor_tensor(out=nmr, in0=mv[:, :, 0], scalar=-1.0, in1=rstd, op0=ALU.mult,
                                         op1=ALU.mult))
            table(v.tensor_tensor(tmp, rstd, rstd, ALU.mult))
            table(v.tensor_tensor(tmp, tmp, mv[:, :, 1], ALU.mult))
            table(v.tensor_scalar(tmp, tmp, EPS, None, ALU.add))
            rooted(3)
            table(v.reciprocal(rms, lcoef))
            rooted(4)
            table(v.tensor_tensor(tmp, ssu, rstd, ALU.mult))
            table(v.tensor_tensor(tmp, tmp, rms, ALU.mult))
            table(v.tensor_scalar(tmp, tmp, EPS, None, ALU.max))
            table(v.reciprocal(tmp, tmp))
            table(v.tensor_tensor(lcoef, tmp, rms, ALU.mult))
            table(v.tensor_scalar(slot_s[:, 1:2], slot_s[:, 1:2], EPS, None, ALU.max))
            table(v.reciprocal(slot_s[:, 2:3], slot_s[:, 1:2]))
            table(v.tensor_scalar(slot_sq, slot_rows, slot_s[:, 2:3], slot_s[:, 3:4], ALU.mult, ALU.mult))
            assert made[0] == SLOTS_AT
            dve.wait_ge(slT_done, 1)
            for k in range(KT):
                last = v.tensor_scalar(slwT[:, k, :], ps_y[0:KP, k * NS:(k + 1) * NS], nw_c[:, k:k + 1], None,
                                       ALU.mult)
            last.then_inc(slwT_ready, 1)

            def token_max(b):
                dve.wait_ge(zT_done, b.n + 1)
                v.tensor_reduce(mxt, bank(2)[0:NS, 0:NTOK], AX_X, ALU.max).then_inc(mxt_ready, 1)
                dve.wait_ge(mxt_ready, b.n + 1)
                v.tensor_scalar(nmt, mxt, -1.0, None, ALU.mult).then_inc(nmt_ready, 1)

            def over_slots(b):
                dve.wait_ge(ez_ready, b.n + 1)
                v.tensor_reduce(sm2, ez[b.par], AX_X, ALU.add).then_inc(sm_ready, 1)
                dve.wait_ge(sm_ready, b.n + 1)
                v.reciprocal(rc2, sm2).then_inc(rc_ready, 1)
                dve.wait_ge(rc_ready, b.n + 1)
                if later(b, 2):
                    dve.wait_ge(e_done, b.n - 1)
                v.tensor_tensor(en[b.par], ez[b.par], rc2.unsqueeze(2).to_broadcast([TP, TT, NS]),
                                ALU.mult).then_inc(en_ready, 1)

            def over_tokens(b):
                dve.wait_ge(pt_ready, b.n + 1)
                v.reciprocal(rzt, zt).then_inc(rzt_ready, 1)
                dve.wait_ge(rzt_ready, b.n + 1)
                if later(b, 2):
                    dve.wait_ge(d_done, b.n - 1)
                v.tensor_scalar(pn[b.par], pt[b.par], rzt, None, ALU.mult).then_inc(pn_ready, 1)

            def dispatch_rows(b):
                dve.wait_ge(d_done, b.n + 1)
                if later(b, 2):
                    dve.wait_ge(y_done, b.n - 1)
                v.tensor_tensor(dr[b.par], tiles(bank(3), TP, NS),
                                rms[:, bass.ds(2 * b.n, 2)].unsqueeze(2).to_broadcast([TP, TT, NS]),
                                ALU.mult).then_inc(dr_ready, 1)

            def logits_out(b):
                dve.wait_ge(lg_done, b.n + 1)
                if later(b, 2):
                    dve.wait_ge(zT_done, b.n - 1)
                v.tensor_tensor(zl[b.par], tiles(bank(1), TP, NS),
                                lcoef[:, bass.ds(2 * b.n, 2)].unsqueeze(2).to_broadcast([TP, TT, NS]),
                                ALU.mult).then_inc(z_ready, 1)
                dve.wait_ge(z_ready, b.n + 1)
                v.tensor_reduce(mx2, zl[b.par], AX_X, ALU.max).then_inc(mx_ready, 1)
                dve.wait_ge(mx_ready, b.n + 1)
                if later(b, 2):
                    dve.wait_ge(ez_ready, b.n - 1)
                v.tensor_tensor(zm[b.par], zl[b.par], mx2.unsqueeze(2).to_broadcast([TP, TT, NS]),
                                ALU.subtract).then_inc(zm_ready, 1)

            def dve_step(s):
                for lag, stage in ((1, logits_out), (3, dispatch_rows), (2, over_tokens), (1, over_slots),
                                   (1, token_max)):
                    if s.has(lag):
                        stage(s.back(lag))

            route(dve, dve_step)

            def hidden_out(j):
                dve.wait_ge(hidT_done, j.n + 1)
                if later(j, 1):
                    dve.wait_ge(fc2_done, j.n)
                v.tensor_copy(hidT, bank(4, 2)[:, 0:F].rearrange("p (k n) -> p k n", k=FK)
                              ).then_inc(hidT_ready, 1)

            def y2_rows(j, fresh=False):
                dve.wait_ge(fc2_done, j.n + 1)
                dve.wait_ge(b2_in[j.par], 32 * (j.half + 1))
                if not fresh:
                    dve.wait_ge(y2_out[j.par], 32 * j.half)
                v.tensor_tensor(y2o[j.par], bank(6)[:, 0:D], b2_s[j.par], ALU.add).then_inc(y2_ready, 1)

            def expert(j, fresh=False):
                hidden_out(j)
                y2_rows(j, fresh)

            expert(at(0), True)
            expert(at(1), True)
            with dve.Fori(1, NPAIR // 2) as i:
                expert(At(2 * i, i, 0))
                expert(At(2 * i + 1, i, 1))

            def pair(i, first=False, last=False, fresh=False):
                if not last:
                    dve.wait_ge(cm_done, i.n + 1)
                    if not fresh:
                        dve.wait_ge(ob_ready, i.n - 1)
                    v.tensor_tensor(rf[i.par].rearrange("p (e t) d -> p e (t d)", e=2),
                                    bank(2 * i.par, 2).rearrange("p (e n) -> p e n", e=2)[0:TP, :, 0:TT * D],
                                    res[:, bass.ds(4 * i.n, 4), :].rearrange("p (e t) d -> p e (t d)", e=2),
                                    ALU.add).then_inc(rf_ready, 1)
                if not first:
                    b = prv(i)
                    dve.wait_ge(sd4_ready, b.n + 1)
                    v.reciprocal(rs4[b.par], sd4[b.par]).then_inc(rs4_ready, 1)
                if not last:
                    dve.wait_ge(rf_ready, i.n + 1)
                    for t in range(4):
                        last_op = v.bn_stats(st4[:, t, :], rf[i.par][:, t, :])
                    last_op.then_inc(st4_ready, 1)
                if not first:
                    dve.wait_ge(rs4_ready, b.n + 1)
                    v.scalar_tensor_tensor(out=nm4[b.par], in0=mv4[b.par][:, :, 0], scalar=-1.0, in1=rs4[b.par],
                                           op0=ALU.mult, op1=ALU.mult).then_inc(nm4_ready, 1)
                if not last:
                    apart(dve, vz_zero, 1)
                    dve.wait_ge(st4_ready, i.n + 1)
                    for t in range(4):
                        last_op = v.bn_aggr(mv4[i.par][:, t, :], st4[:, t, :])
                    last_op.then_inc(mv4_ready, 1)
                    dve.wait_ge(mv4_ready, i.n + 1)
                    if not fresh:
                        dve.wait_ge(sd4_ready, i.n - 1)
                    v.tensor_scalar(ve4[i.par], mv4[i.par][:, :, 1], EPS, None, ALU.add).then_inc(ve4_ready, 1)

            dve.wait_ge(yst_ready, NPAIR)
            pair(at(0), first=True, fresh=True)
            pair(at(1), fresh=True)
            with dve.Fori(1, NB // 4) as i:
                pair(At(2 * i, i, 0))
                pair(At(2 * i + 1, i, 1))
            pair(at(NB // 2), last=True)


def kernel(**inputs):
    import numpy as np
    import concourse.bacc as bacc
    from concourse.bass_utils import run_bass_kernel_spmd

    a = {k: np.asarray(val) for k, val in inputs.items()}
    side, p = a["x"].shape[2] // 16, 16

    def rows(w, tiles):
        return w.reshape(tiles, w.shape[0] // tiles, -1).transpose(1, 0, 2)

    x = a["x"].reshape(NB, 3, side, p, side, p).transpose(0, 1, 3, 5, 2, 4)
    arrays = {
        "x": x.reshape(NB, PK, 128, NTOK).transpose(0, 2, 1, 3),
        "wp": rows(a["L0_tok_Wp"].T, PK),
        "bp": a["L0_tok_bp"].reshape(KT, KP).T,
        "attn_bias": a["L0_attn_bias"].reshape(1, 1),
        "wq": rows(a["L0_attn_Wq"].T, KT),
        "bq": a["L0_attn_bq"].reshape(KT, KP).T,
        "wk": rows(a["L0_attn_Wk"].T, KT),
        "bk": a["L0_attn_bk"].reshape(KT, KP).T,
        "wv": rows(a["L0_attn_Wv"].T, KT),
        "bv": a["L0_attn_bv"],
        "wo": rows(a["L0_attn_Wo"].T, KT),
        "bo": a["L0_attn_bo"],
        "slots": a["L0_ffn_slots"],
        "scale": a["L0_ffn_scale"].reshape(NS, 1),
        "w1": a["L0_ffn_fc1_weight"].reshape(NS, KT, KP, F).transpose(0, 2, 1, 3),
        "b1": a["L0_ffn_fc1_bias"],
        "w2": a["L0_ffn_fc2_weight"].reshape(NS, FK, 128, D).transpose(0, 2, 1, 3),
        "b2": a["L0_ffn_fc2_bias"],
        "norm_w": a["L0_ffn_norm_weight"],
        "norm_c": a["L0_ffn_norm_weight"].reshape(KT, KP).T,
        "ident": np.eye(128, dtype=np.float32),
    }
    nc = bacc.Bacc("TRN2", target_bir_lowering=False, num_devices=1)
    feeds, aps = {}, []
    for name, arr in arrays.items():
        arr = np.ascontiguousarray(arr)
        feeds[f"in_{name}"] = arr
        aps.append(nc.dram_tensor(f"in_{name}", arr.shape, mybir.dt.from_np(arr.dtype), kind="ExternalInput").ap())
    out = nc.dram_tensor("out", (NB, NTOK, D), F32, kind="ExternalOutput").ap()
    vit_tower(nc, *aps, out)
    r = run_bass_kernel_spmd(nc, [feeds], core_ids=[0])
    return r.results[0]["out"]
```

```python
from contextlib import ExitStack
from collections import namedtuple

import concourse.bass as bass
from concourse import mybir

F32 = mybir.dt.float32
BF16 = mybir.dt.bfloat16
ALU = mybir.AluOpType
ACT = mybir.ActivationFunctionType
AX_X = mybir.AxisListType.X

NB, NTOK, D = 64, 196, 192
PATCH = 768
HEADS, HD = 12, 16
NS, F = 64, 768
TT = 2
TP = NTOK // TT
KT = 2
KP = D // KT
PK = PATCH // 128
FK = F // 128
PAIRS = HEADS // 2
STRIPS = 4
MT = 3
HPT = HEADS // MT
PARTS = 3
Q_STACK, K_STACK = (0, 0, 0, 1, 1, 2), (0, 1, 2, 0, 1, 0)
STACK = len(Q_STACK) * HD
EPS = 1e-5
BANK = 512
SBUF_WORDS = 53200
NPAIR = NS // 2

At = namedtuple("At", "n half par")


def nxt(b):
    return At(b.n + 1, b.half + b.par % 2, (b.par + 1) % 2)


def prv(b):
    return At(b.n - 1, b.half - 1 + b.par % 2, (b.par + 1) % 2)


def at(n):
    return At(n, n // 2, n % 2)


def later(b, n):
    return not isinstance(b.n, int) or b.n >= n


def apart(engine, done, value):
    engine.wait_ge(done, value)


SLOTS_AT = 4
LCOEF_AT = 10
RING = 4
LOWEST = -3.4028234e38
Ringed = namedtuple("Ringed", "n half par turn ring")


def ringed(i, u):
    return Ringed(RING * i + u, 2 * i + u // 2, u % 2, i + u // RING, u % RING)


class Step:

    def __init__(self, i, u):
        self.i, self.u = i, u

    def has(self, lag):
        return not isinstance(self.i, int) or 0 <= RING * self.i + self.u - lag < NPAIR

    def back(self, lag):
        return ringed(self.i, self.u - lag)


def route(engine, step):
    for n in range(-1, 2 * RING):
        step(Step(n // RING, n % RING))
    with engine.Fori(2, NPAIR // RING - 1) as i:
        for u in range(RING):
            step(Step(i, u))
    for u in range(RING + 4):
        step(Step(NPAIR // RING - 1, u))


class Layout:

    def __init__(self, arena, start):
        self.arena, self.at = arena, start

    def take(self, parts, *dims):
        size = 1
        for d in dims:
            size *= d
        ap = self.arena[0:parts, self.at:self.at + size]
        self.at += size
        assert self.at <= SBUF_WORDS, self.at
        names = "abcde"[:len(dims)]
        if len(dims) > 1:
            kw = {n: d for n, d in zip(names, dims)}
            ap = ap.rearrange(f"p ({' '.join(names)}) -> p {' '.join(names)}", **kw)
        return ap

    def take_bf16(self, parts, *dims):
        size = 1
        for d in dims:
            size *= d
        names = "abcde"[:len(dims)]
        kw = {n: d for n, d in zip(names, dims)}
        return self.take(parts, size // 2).bitcast(BF16).rearrange(
            f"p ({' '.join(names)}) -> p {' '.join(names)}", **kw)


def vit_tower(nc, x, wp, bp, attn_bias, wqk, bqk, wv, bv, wo, bo, slots, scale, w1, w2, b2,
              norm_w, norm_c, ident_d, out):
    qk_dram = nc.dram_tensor("qk_parts", (2, MT, PARTS, 128, NTOK), BF16, kind="Internal").ap()
    lc_dram = nc.dram_tensor("logit_coefficients", (NB, NTOK), F32, kind="Internal").ap()
    y2_dram = nc.dram_tensor("slot_outputs", (NPAIR, 2, NB, D), F32, kind="Internal").ap()

    with ExitStack() as ctx:
        def sem(name):
            return ctx.enter_context(nc.semaphore(name))

        arena = ctx.enter_context(nc.sbuf_tensor("arena", [128, SBUF_WORDS], F32))
        psum = ctx.enter_context(nc.psum_tensor("psum", [128, 8 * BANK], F32))

        def bank(i, n=1):
            return psum[:, i * BANK:(i + n) * BANK]

        keep = Layout(arena, 0)
        res = keep.take(TP, NB * TT, D)
        ident = keep.take(128, 128)
        abias, eps_c = keep.take(TP, 1), keep.take(TP, 1)
        bp_c = keep.take(128, 2)
        nw_c = keep.take(KP, KT)
        bqk_c = keep.take(128, MT)
        slwT = keep.take(KP, KT, NS)
        tables_at = keep.at
        tab = Layout(arena, tables_at)
        mv = tab.take(TP, NB * TT, 2)
        ssu = tab.take(TP, NB * TT)
        rstd, nmr, rms, lcoef, tmp = (tab.take(TP, NB * TT) for _ in range(5))
        slot_rows = tab.take(NS, D)
        slot_sq = tab.take(NS, D)
        slot_s = tab.take(NS, 4)
        lcT = tab.take(NB * TT, TP)
        y_words, c_words, w_words = KT * NB * NS, NPAIR * NTOK, 2 * KT * F + 2 * FK * D
        big_at = SBUF_WORDS - (y_words + c_words + 2 * w_words)
        big = Layout(arena, big_at)
        comb = big.take(128, NPAIR, NTOK)
        yT = big.take(KP, KT, NB, NS)
        w_at = big.at
        w1_s, w2_s = [], []
        for _ in range(2):
            w1_s.append(big.take(KP + 1, 2, 2, KT, F // 2))
            w2_s.append(big.take(128, 2, FK, D))
        assert tab.at <= big_at

        p1 = Layout(arena, big_at)
        xs = [p1.take(128, PK, NTOK) for _ in range(2)]
        wp_s = p1.take(128, PK, D)
        wqk_s = p1.take(KP, KT, MT * 128)
        wv_s = p1.take(KP, KT, D)
        wo_s = p1.take(128, 2, D)
        hT = [p1.take(KP, KT, NTOK) for _ in range(2)]
        parts = [p1.take_bf16(128, n, PARTS, NTOK) for n in (2, 1)]
        rest = [p1.take(128, n, NTOK) for n in (2, 1)]
        stacks = [[p1.take_bf16(STACK, HEADS, NTOK) for _ in range(2)] for _ in range(2)]
        vz = [p1.take(TP, TT, PAIRS * 4, HD) for _ in range(2)]
        sig = p1.take(TP, PAIRS, 2, TT, NTOK)
        aT = p1.take(128, 2, NTOK)
        hb = [p1.take(TP, TT, D) for _ in range(2)]
        bv_b, bo_b, nw_b = (p1.take(TP, TT, D) for _ in range(3))
        rt = [p1.take(TP, TT, D) for _ in range(2)]
        ut = p1.take(TP, TT, D)
        st = p1.take(TP, TT, 6)
        mvt = [p1.take(TP, TT, 2) for _ in range(2)]
        sst = [p1.take(TP, TT) for _ in range(2)]

        w1_words = 2 * KT * F
        p2 = Layout(arena, w_at + w1_words)
        h1s = [p2.take(TP, 2, TT, D) for _ in range(RING)]
        hT2 = [p2.take(KP, 2, KT, NTOK) for _ in range(2)]
        lcb = [p2.take(128, NTOK) for _ in range(2)]
        zs = [p2.take(128, NTOK) for _ in range(2)]
        pt = [p2.take(128, NTOK) for _ in range(2)]
        ez = [p2.take(TP, TT, 2 * NS) for _ in range(2)]
        dr = [p2.take(TP, TT, 2, NS) for _ in range(2)]
        ys = [p2.take(128, D) for _ in range(2)]
        mx2, sm2, rc2 = (p2.take(TP, TT * 2) for _ in range(3))
        mxt, nmt, zt, rzt = ([p2.take(128, 1) for _ in range(2)] for _ in range(4))

        p3 = Layout(arena, tables_at)
        hid = p3.take(128, F)
        hidT = p3.take(128, FK, 128)
        yst = [p3.take(KP + 1, KT, 2, NB) for _ in range(2)]
        y2o = [p3.take(128, D) for _ in range(2)]
        b2_s = p3.take(128, D)
        assert p3.at <= big_at

        p4 = Layout(arena, big_at + c_words)
        y2s = [p4.take(128, D) for _ in range(RING)]
        cst = [p4.take(128, NTOK) for _ in range(RING)]
        rf = [p4.take(TP, 4, D) for _ in range(RING)]
        ob = [p4.take(TP, 4, D) for _ in range(RING)]
        st4 = p4.take(TP, 4, 6)
        mv4 = [p4.take(TP, 4, 2) for _ in range(RING)]
        sd4, rs4, nm4 = ([p4.take(TP, 4) for _ in range(RING)] for _ in range(3))
        assert p4.at <= w_at

        ps_sc = [bank(0, 2).rearrange("p (h n) -> p h n", h=2), bank(2, 2).rearrange("p (h n) -> p h n", h=2)]
        ps_av, ps_x, ps_y, ps_z = bank(4), bank(5), bank(6), bank(7)

        def tiles(b, p, n):
            return b[0:p, 0:2 * n].rearrange("p (t n) -> p t n", t=2)

        emb_in, qk_in, const_in = sem("emb_in"), sem("qk_in"), sem("const_in")
        x_in = [sem("x_in0"), sem("x_in1")]
        (tok_done, hT_ready, qk01_done, qk2_done, qk01_high, qk2_high, qk01_rest, qk2_rest, qk01_mid,
         qk2_mid, qk01_parts, qk2_parts, v_done, v_ready, tr_done, hb_ready, sc_done, sig_done, av_done,
         aT_ready, o_done, r_ready, st_ready, mv_ready, u_ready, ss_ready, kept) = (sem(n) for n in (
             "tok_done", "hT_ready", "qk01_done", "qk2_done", "qk01_high", "qk2_high", "qk01_rest",
             "qk2_rest", "qk01_mid", "qk2_mid", "qk01_parts", "qk2_parts", "v_done", "v_ready", "tr_done",
             "hb_ready", "sc_done", "sig_done", "av_done", "aT_ready", "o_done", "r_ready", "st_ready",
             "mv_ready", "u_ready", "ss_ready", "kept"))
        vz_zero, next_ready = sem("vz_zero"), sem("next_ready")
        parts_out = [sem("qk01_parts_out"), sem("qk2_parts_out")]
        stack_in = [sem("stack_in0"), sem("stack_in1")]
        slots_dve, tables_dve, tables_act, slT_done, slwT_ready = (sem(n) for n in (
            "slots_dve", "tables_dve", "tables_act", "slT_done", "slwT_ready"))
        lcT_done, lcT_ready, lc_out = sem("lcT_done"), sem("lcT_ready"), sem("lc_out")
        lc_in = [sem("lc_in0"), sem("lc_in1")]
        h1_ready = [sem("h1_ready0"), sem("h1_ready1")]
        (h1_kept, hT2_done, hT2_ready, lg_done, zs_ready, nmt_ready, zr_done, mx_ready, zm_ready,
         ez_ready, sm_ready, rc_ready, en_ready, pt_ready, rzt_ready, d_done, dr_ready, e_done,
         comb_ready, y_done, ys_ready, yT_done, yT_ready) = (sem(n) for n in (
             "h1_kept", "hT2_done", "hT2_ready", "lg_done", "zs_ready", "nmt_ready", "zr_done",
             "mx_ready", "zm_ready", "ez_ready", "sm_ready", "rc_ready", "en_ready", "pt_ready",
             "rzt_ready", "d_done", "dr_ready", "e_done", "comb_ready", "y_done", "ys_ready",
             "yT_done", "yT_ready"))
        w1_in = [[sem(f"w1_in{q}_{half}") for half in range(2)] for q in range(2)]
        w2_in = [[sem(f"w2_in{q}_{half}") for half in range(2)] for q in range(2)]
        b2_in, y2_biased = sem("b2_in"), sem("y2_biased")
        (yst_ready, ones_set, fc1_half, fc1_done, hid_ready, hidT_done, hidT_ready, fc2_half, fc2_done,
         y2_ready) = (sem(n) for n in (
             "yst_ready", "ones_set", "fc1_half", "fc1_done", "hid_ready", "hidT_done", "hidT_ready",
             "fc2_half", "fc2_done", "y2_ready"))
        y2_out = [sem("y2_out0"), sem("y2_out1")]
        y2_in = [sem(f"y2_in{u}") for u in range(RING)]
        (cst_ready, cm_done, rf_ready, st4_ready, mv4_ready, sd4_ready, rs4_ready, nm4_ready, ob_ready) = (
            sem(n) for n in ("cst_ready", "cm_done", "rf_ready", "st4_ready", "mv4_ready", "sd4_ready",
                             "rs4_ready", "nm4_ready", "ob_ready"))
        out_done = [sem(f"out_done{u}") for u in range(RING)]

        consts = [
            (wv_s, wv), (wo_s, wo), (ident, ident_d), (nw_c, norm_c),
            (abias, attn_bias.to_broadcast([TP, 1])),
            (slot_rows, slots), (slot_s[:, 3:4], scale),
        ]
        for tile, row in ((bv_b, bv), (bo_b, bo), (nw_b, norm_w)):
            for t in range(TT):
                consts.append((tile[:, t, :], row.rearrange("(a d) -> a d", a=1).to_broadcast([TP, D])))
        CONSTS = 16 * len(consts)

        out_v = out.rearrange("b (t p) d -> p (b t) d", p=TP)
        block = ctx.enter_context(nc.Block())

        @block.sync
        def _(sp):
            def load_x(b):
                sp.wait_ge(tok_done, b.n - 1)
                sp.dma_start(xs[b.par], x[bass.ds(b.n, 1)].rearrange("a p k n -> (a p) k n")
                             ).then_inc(x_in[b.par], 16)

            def step(b, more=True, fresh=False):
                for w, made in ((0, qk01_parts), (1, qk2_parts)):
                    if w == 0 and not fresh:
                        sp.wait_ge(stack_in[b.par], 16 * 2 * len(Q_STACK) * b.half)
                    sp.wait_ge(made, b.n + 1)
                    sp.dma_start(qk_dram[b.par, (0, 2)[w]:(2, MT)[w]].rearrange("m c p n -> p (m c) n"),
                                 parts[w].rearrange("p m c n -> p (m c) n")).then_inc(parts_out[w], 16)
                if more:
                    load_x(nxt(nxt(nxt(b))))
                if not fresh:
                    sp.wait_ge(sc_done, PAIRS * (b.n - 1))
                for landed in parts_out:
                    sp.wait_ge(landed, 16 * b.n + 16)
                for w, order in ((0, Q_STACK), (1, K_STACK)):
                    src = qk_dram[b.par].rearrange("m c (w f h) n -> c w f m (h n)", w=2, f=HD)
                    for i, part in enumerate(order):
                        sp.dma_start(stacks[w][b.par][HD * i:HD * (i + 1)].rearrange("p (m h) n -> p m (h n)", m=MT),
                                     src[part, w]).then_inc(stack_in[b.par], 16)

            sp.dma_start(xs[0], x[0]).then_inc(x_in[0], 16)
            for tile, src in ((wp_s, wp), (bp_c, bp)):
                sp.dma_start(tile, src).then_inc(emb_in, 16)
            sp.dma_start(xs[1], x[1]).then_inc(x_in[1], 16)
            for tile, src in ((wqk_s, wqk), (bqk_c, bqk)):
                sp.dma_start(tile, src).then_inc(qk_in, 16)
            for tile, src in consts:
                sp.dma_start(tile, src).then_inc(const_in, 16)
            load_x(at(2))
            step(at(0), fresh=True)
            step(at(1), fresh=True)
            with sp.Fori(1, NB // 2 - 2) as i:
                step(At(2 * i, i, 0))
                step(At(2 * i + 1, i, 1))
            step(at(NB - 4))
            for n in range(NB - 3, NB):
                step(at(n), more=False)

            def load_w1(j):
                for half, used in enumerate((fc1_half, fc1_done)):
                    if later(j, 2):
                        sp.wait_ge(used, j.n - 1)
                    sp.dma_start(w1_s[j.par][:, half].rearrange("p s k f -> p s (k f)"),
                                 w1[bass.ds(2 * j.n, 2), half].rearrange("s p k f -> p s (k f)")
                                 ).then_inc(w1_in[j.par][half], 16)

            def load_w2(j):
                for half, used in enumerate((fc2_half, fc2_done)):
                    if later(j, 2):
                        sp.wait_ge(used, j.n - 1)
                    ks = slice(half * (FK // 2), (half + 1) * (FK // 2))
                    sp.dma_start(w2_s[j.par][:, :, ks, :].rearrange("p s k d -> p s (k d)"),
                                 w2[bass.ds(2 * j.n, 2), :, ks, :].rearrange("s p k d -> p s (k d)")
                                 ).then_inc(w2_in[j.par][half], 16)

            def store_y2(j):
                sp.wait_ge(y2_ready, j.n + 1)
                sp.dma_start(y2_dram[bass.ds(j.n, 1)].rearrange("a s b d -> (a s b) d"), y2o[j.par]
                             ).then_inc(y2_out[j.par], 16)

            def load_lc(p):
                if later(p, 2):
                    sp.wait_ge(zs_ready, p.n - 1)
                for u in range(2):
                    sp.dma_start(lcb[p.par][NS * u:NS * u + NS, :],
                                 lc_dram[bass.ds(2 * p.n + u, 1), :].to_broadcast([NS, NTOK])
                                 ).then_inc(lc_in[p.par], 16)

            sp.wait_ge(kept, 3 * NB)
            load_w1(at(0))
            sp.wait_ge(lcT_ready, 1)
            sp.dma_start(lc_dram.rearrange("b (t p) -> (b t) p", p=TP), lcT).then_inc(lc_out, 16)
            sp.wait_ge(lc_out, 16)
            load_lc(at(0))
            load_lc(at(1))
            with sp.Fori(1, NPAIR // 2) as i:
                load_lc(At(2 * i, i, 0))
                load_lc(At(2 * i + 1, i, 1))
            sp.wait_ge(yT_ready, NPAIR)
            sp.wait_ge(comb_ready, NPAIR)
            sp.wait_ge(h1_kept, NPAIR)
            load_w2(at(0))
            load_w1(at(1))
            load_w2(at(1))
            for e in range(2):
                sp.dma_start(b2_s[NS * e:NS * e + NS, :], b2).then_inc(b2_in, 16)
            load_w1(at(2))

            def step(j, w1_too=True):
                ahead = nxt(nxt(j))
                if w1_too:
                    load_w1(nxt(ahead))
                load_w2(ahead)
                store_y2(j)

            with sp.Fori(0, NPAIR // 2 - 2) as i:
                step(At(2 * i, i, 0))
                step(At(2 * i + 1, i, 1))
            step(at(NPAIR - 4))
            step(at(NPAIR - 3), w1_too=False)
            for n in (NPAIR - 2, NPAIR - 1):
                store_y2(at(n))

            for s in y2_out:
                sp.wait_ge(s, 16 * (NPAIR // 2))
            def load_y2(i):
                if later(i, RING):
                    sp.wait_ge(cm_done, i.n - RING + 1)
                for e in range(2):
                    sp.dma_start(y2s[i.ring][NS * e:NS * e + NS, :],
                                 y2_dram[:, :, bass.ds(2 * i.n + e, 1), :].rearrange("j s a d -> (j s a) d")
                                 ).then_inc(y2_in[i.ring], 16)

            for u in range(RING):
                load_y2(ringed(0, u))
            with sp.Fori(1, NPAIR // RING) as i:
                for u in range(RING):
                    load_y2(ringed(i, u))
            for s in out_done:
                sp.wait_ge(s, 16 * (NPAIR // RING))

        @block.tensor
        def _(pe):
            mm, tr = nc.tensor.matmul, nc.tensor.transpose

            def tok(b, part):
                if part == 0:
                    if b.par == 0:
                        pe.wait_ge(x_in[0], 16 * (b.half + 1))
                    if later(b, 2):
                        pe.wait_ge(v_ready, b.n)
                    elif b.n == 1:
                        pe.wait_ge(hT_ready, 1)
                        pe.wait_ge(next_ready, 1)
                if b.par == 1 or part == 0:
                    ks = range(PK) if b.par == 0 else range(part * (PK // 2), (part + 1) * (PK // 2))
                    for k in ks:
                        last = mm(ps_x[:, 0:NTOK], wp_s[:, k, 0:128], xs[b.par][:, k, :],
                                  start=k == 0, stop=k == PK - 1)
                else:
                    pe.wait_ge(x_in[1], 16 * (b.half + 1))
                    for k in range(PK):
                        for u in range(2):
                            last = mm(ps_x[64 * u:64 * u + 64, NTOK:2 * NTOK], wp_s[:, k, 128:D], xs[u][:, k, :],
                                      start=k == 0, stop=k == PK - 1)
                if part == 1:
                    last.then_inc(tok_done, 1)

            def qk_tiles(b, tiles_in, bankap, done):
                for i, m in enumerate(tiles_in):
                    for k in range(KT):
                        last = mm(bankap[:, i * NTOK:(i + 1) * NTOK], wqk_s[:, k, m * 128:(m + 1) * 128],
                                  hT[b.par][:, k, :], start=k == 0, stop=k == KT - 1)
                last.then_inc(done, 1)

            def qk01(b):
                pe.wait_ge(hT_ready, b.n + 1)
                if later(b, 3):
                    pe.wait_ge(r_ready, b.n - 2)
                elif b.n == 1:
                    pe.wait_ge(qk01_rest, 1)
                qk_tiles(b, (0, 1), ps_y, qk01_done)

            def qk2(b):
                if later(b, 2):
                    pe.wait_ge(hb_ready, b.n)
                elif b.n == 1:
                    pe.wait_ge(qk2_rest, 1)
                qk_tiles(b, (2,), ps_z, qk2_done)

            def by_token(lhs, w, bankap, done):
                o = tiles(bankap, TP, D)
                for t in range(TT):
                    for k in range(KT):
                        last = mm(o[:, t, :], lhs[:, k, t * TP:(t + 1) * TP], w[:, k, :],
                                  start=k == 0, stop=k == KT - 1)
                last.then_inc(done, 1)

            def values(b):
                if not later(b, 1):
                    pe.wait_ge(hT_ready, 2)
                if b.par == 0:
                    pe.wait_ge(next_ready, b.half + 1)
                if not later(b, 2) and b.n == 1:
                    pe.wait_ge(v_ready, 1)
                by_token(hT[b.par], wv_s, ps_x, v_done)

            def h_transposed1(b):
                pe.wait_ge(qk2_rest, max(b.n + 1, 2) if isinstance(b.n, int) else b.n + 1)
                if not later(b, 2) and b.n == 1:
                    pe.wait_ge(hb_ready, 1)
                o = tiles(ps_z, TP, D)
                for t in range(TT):
                    for k in range(KT):
                        last = tr(o[:, t, k * KP:(k + 1) * KP], hT[b.par][:, k, t * TP:(t + 1) * TP],
                                  ident[0:KP, 0:KP])
                last.then_inc(tr_done, 1)

            def scores(b, g):
                if g == 0:
                    pe.wait_ge(stack_in[b.par], 16 * 2 * len(Q_STACK) * (b.half + 1))
                if g >= 2:
                    pe.wait_ge(sig_done, 6 * b.n + g - 1)
                q_st, k_st = stacks[0][b.par], stacks[1][b.par]
                for a in range(2):
                    h = 2 * g + a
                    for t in range(TT):
                        last = mm(ps_sc[g % 2][0:TP, a, t * NTOK:(t + 1) * NTOK],
                                  k_st[:, h, t * TP:(t + 1) * TP], q_st[:, h, :],
                                  start=True, stop=True)
                last.then_inc(sc_done, 1)

            def attend(b, half):
                pe.wait_ge(sig_done, 6 * b.n + (4, 6)[half])
                if half == 0 and isinstance(b.n, int):
                    pe.wait_ge(v_ready, b.n + 1)

                def strip(c, g, a, t, start, stop):
                    vt = vz[b.par][:, t, 4 * g + 2 * a:4 * g + 2 * a + 2, :]
                    return mm(ps_av[32 * c:32 * c + 32, half * NTOK:(half + 1) * NTOK],
                              vt.rearrange("p a f -> p (a f)"), sig[:, g, a, t, :], start=start, stop=stop)

                if half == 0:
                    for a in range(2):
                        for t in range(TT):
                            for c in range(STRIPS):
                                last = strip(c, c, a, t, a == 0 and t == 0, a == 1 and t == TT - 1)
                else:
                    for t in range(TT):
                        for c in range(STRIPS):
                            last = strip(c, STRIPS + c // 2, c % 2, t, t == 0, t == TT - 1)
                last.then_inc(av_done, 1)

            def o_proj(b):
                pe.wait_ge(aT_ready, b.n + 1)
                pe.wait_ge(qk01_rest, min(b.n + 3, NB) if isinstance(b.n, int) else b.n + 3)
                if isinstance(b.n, int) and b.n >= NB - 2:
                    pe.wait_ge(r_ready, b.n)
                by_token(aT, wo_s, ps_y, o_done)

            def step(b, first=False, project_next=True, value_next=True):
                ahead = nxt(nxt(b))
                if not first:
                    attend(prv(b), 1)
                if value_next:
                    values(nxt(b))
                    h_transposed1(nxt(b))
                scores(b, 0)
                scores(b, 1)
                if project_next:
                    tok(ahead, 0)
                scores(b, 2)
                if project_next:
                    tok(ahead, 1)
                scores(b, 3)
                if not first:
                    o_proj(prv(b))
                scores(b, 4)
                attend(b, 0)
                scores(b, 5)
                if project_next:
                    qk01(ahead)
                    qk2(ahead)

            pe.wait_ge(emb_in, 32)
            for n in range(2):
                for part in range(2):
                    tok(at(n), part)
                if n == 0:
                    pe.wait_ge(qk_in, 32)
                qk01(at(n))
                qk2(at(n))
            pe.wait_ge(const_in, CONSTS)
            values(at(0))
            h_transposed1(at(0))
            step(at(0), first=True)
            with pe.Fori(0, NB // 2 - 2) as i:
                step(At(2 * i + 1, i, 1))
                step(At(2 * i + 2, i + 1, 0))
            step(at(NB - 3))
            step(at(NB - 2), project_next=False)
            step(at(NB - 1), project_next=False, value_next=False)
            attend(at(NB - 1), 1)
            o_proj(at(NB - 1))

            pe.wait_ge(r_ready, NB)
            pe.wait_ge(slots_dve, SLOTS_AT)
            for k in range(KT):
                last = tr(ps_y[0:KP, k * NS:(k + 1) * NS], slot_sq[:, k * KP:(k + 1) * KP], ident[0:NS, 0:NS])
            last.then_inc(slT_done, 1)
            pe.wait_ge(hb_ready, NB)
            pe.wait_ge(tables_dve, LCOEF_AT)
            tr(ps_z[0:NB * TT, 0:TP], lcoef, ident[0:TP, 0:TP]).then_inc(lcT_done, 1)
            pe.wait_ge(slwT_ready, 1)

            def h_transposed(p):
                for s in h1_ready:
                    pe.wait_ge(s, p.n + 1)
                if later(p, 1):
                    pe.wait_ge(hT2_ready, p.n)
                for u in range(2):
                    o = tiles(bank(u), KP, NTOK)
                    for k in range(KT):
                        for t in range(TT):
                            last = tr(o[:, k, t * TP:(t + 1) * TP], h1s[p.ring][:, u, t, k * KP:(k + 1) * KP],
                                      ident[0:TP, 0:TP])
                    last.then_inc(hT2_done, 1)

            def logits(p):
                pe.wait_ge(hT2_ready, p.n + 1)
                if later(p, 1):
                    pe.wait_ge(zs_ready, p.n)
                for k in range(KT):
                    for u in range(2):
                        last = mm(bank(2)[NS * u:NS * u + NS, 0:NTOK], slwT[:, k, :], hT2[p.par][:, u, k, :],
                                  start=k == 0, stop=k == KT - 1)
                last.then_inc(lg_done, 1)

            def logit_rows(p):
                pe.wait_ge(zs_ready, p.n + 1)
                if later(p, 1):
                    pe.wait_ge(zm_ready, p.n)
                for t in range(TT):
                    last = tr(bank(3)[0:TP, 2 * NS * t:2 * NS * (t + 1)], zs[p.par][:, t * TP:(t + 1) * TP], ident)
                last.then_inc(zr_done, 1)

            def weights_transposed(p):
                pe.wait_ge(pt_ready, p.n + 1)
                if later(p, 1):
                    pe.wait_ge(dr_ready, p.n)
                for t in range(TT):
                    last = tr(bank(4)[0:TP, 2 * NS * t:2 * NS * (t + 1)], pt[p.par][:, t * TP:(t + 1) * TP], ident)
                last.then_inc(d_done, 1)
                pe.wait_ge(en_ready, p.n + 1)
                if later(p, 1):
                    pe.wait_ge(comb_ready, p.n)
                for t in range(TT):
                    last = tr(bank(5)[:, t * TP:(t + 1) * TP], ez[p.par][:, t, :], ident[0:TP, 0:TP])
                last.then_inc(e_done, 1)

            def slot_inputs(p):
                pe.wait_ge(dr_ready, p.n + 1)
                if later(p, 1):
                    pe.wait_ge(ys_ready, p.n)
                for t in range(TT):
                    for u in range(2):
                        last = mm(bank(6)[NS * u:NS * u + NS, 0:D], dr[p.par][:, t, u, :], h1s[p.ring][:, u, t, :],
                                  start=t == 0, stop=t == TT - 1)
                last.then_inc(y_done, 1)

            def y_transposed(p):
                pe.wait_ge(ys_ready, p.n + 1)
                if later(p, 1):
                    pe.wait_ge(yT_ready, p.n)
                for k in range(KT):
                    last = tr(bank(7)[0:KP, 2 * NS * k:2 * NS * (k + 1)], ys[p.par][:, k * KP:(k + 1) * KP], ident)
                last.then_inc(yT_done, 1)

            def pe_step(s):
                for lag, stage in ((3, weights_transposed), (1, logits), (4, y_transposed), (0, h_transposed),
                                   (3, slot_inputs), (1, logit_rows)):
                    if s.has(lag):
                        stage(s.back(lag))

            route(pe, pe_step)

            pe.wait_ge(yT_ready, NPAIR)
            pe.wait_ge(comb_ready, NPAIR)
            pe.wait_ge(ones_set, 2)

            def fc1(j, fresh=False):
                pe.wait_ge(yst_ready, j.n + 1)
                if not fresh:
                    pe.wait_ge(hid_ready, j.n - 1)
                for half in range(2):
                    pe.wait_ge(w1_in[j.par][half], 16 * (j.half + 1))
                    for k in range(KT):
                        K = KP + 1 if k == KT - 1 else KP
                        for s in range(2):
                            last = mm(bank(2 * j.par + half)[64 * s:64 * s + 64, 0:F // 2],
                                      yst[j.par][0:K, k, s, :],
                                      w1_s[j.par][0:K, half, s, k, :],
                                      start=k == 0, stop=k == KT - 1)
                    last.then_inc((fc1_half, fc1_done)[half], 1)

            def hidden_transposed(j):
                pe.wait_ge(hid_ready, j.n + 1)
                if later(j, 1):
                    pe.wait_ge(hidT_ready, j.n)
                for k in range(FK):
                    last = tr(bank(4, 2)[:, k * 128:(k + 1) * 128], hid[:, k * 128:(k + 1) * 128], ident)
                last.then_inc(hidT_done, 1)

            def fc2(j):
                pe.wait_ge(hidT_ready, j.n + 1)
                if later(j, 1):
                    pe.wait_ge(y2_ready, j.n)
                for half in range(2):
                    pe.wait_ge(w2_in[j.par][half], 16 * (j.half + 1))
                    for k in range(half * (FK // 2), (half + 1) * (FK // 2)):
                        for s in range(2):
                            last = mm(bank(6)[64 * s:64 * s + 64, 0:D], hidT[:, k, 64 * s:64 * s + 64],
                                      w2_s[j.par][:, s, k, :], start=k == 0, stop=k == FK - 1)
                    last.then_inc((fc2_half, fc2_done)[half], 1)

            def expert(j, last=False, fresh=False):
                hidden_transposed(j)
                if not last:
                    fc1(nxt(j), fresh)
                fc2(j)

            fc1(at(0), fresh=True)
            expert(at(0), fresh=True)
            with pe.Fori(0, NPAIR // 2 - 1) as i:
                expert(At(2 * i + 1, i, 1))
                expert(At(2 * i + 2, i + 1, 0))
            expert(at(NPAIR - 1), last=True)

            def combine(i):
                pe.wait_ge(y2_biased, i.n + 1)
                pe.wait_ge(cst_ready, i.n + 1)
                if later(i, RING):
                    pe.wait_ge(rf_ready, i.n - RING + 1)
                for t in range(TT):
                    for e in range(2):
                        last = mm(bank(2 * i.ring + e)[0:TP, t * D:(t + 1) * D],
                                  cst[i.ring][64 * e:64 * e + 64, t * TP:(t + 1) * TP],
                                  y2s[i.ring][64 * e:64 * e + 64, :], start=True, stop=True)
                last.then_inc(cm_done, 1)

            pe.wait_ge(hid_ready, NPAIR)
            pe.wait_ge(y2_ready, NPAIR)
            for u in range(RING):
                combine(ringed(0, u))
            with pe.Fori(1, NPAIR // RING) as i:
                for u in range(RING):
                    combine(ringed(i, u))

        @block.scalar
        def _(act):
            fn = nc.scalar.activation

            def sigmoid(b, g, first=False):
                act.wait_ge(sc_done, 6 * b.n + g + 1)
                if not first:
                    act.wait_ge(av_done, 2 * b.n + g // STRIPS - 1)
                fn(sig[:, g].rearrange("p a t n -> p a (t n)"), ps_sc[g % 2][0:TP, :, 0:TT * NTOK],
                   ACT.Sigmoid, bias=abias, scale=float(D) ** -0.5).then_inc(sig_done, 1)

            def h_out(b):
                act.wait_ge(tok_done, b.n + 1)
                if later(b, 2):
                    act.wait_ge(tr_done, b.n)
                moves = [(slice(0, KP), 0, slice(0, KP), 0), (slice(64, KP), 1, slice(KP, 128), 0)]
                if b.par == 0:
                    moves.append((slice(0, 64), 1, slice(0, 64), 1))
                for dst, tile, src, part in moves:
                    last = fn(hT[b.par][dst, tile, :], ps_x[src, part * NTOK:(part + 1) * NTOK], ACT.Identity,
                              bias=bp_c[src, part:part + 1])
                last.then_inc(hT_ready, 1)

            def attention_out(b, fresh=False):
                act.wait_ge(av_done, 2 * b.n + 2)
                if not fresh:
                    act.wait_ge(o_done, b.n)
                fn(aT, tiles(ps_av, 128, NTOK), ACT.Copy).then_inc(aT_ready, 1)

            def next_h_out(b):
                fn(hT[1][0:64, 1, :], ps_x[64:128, NTOK:2 * NTOK], ACT.Identity,
                   bias=bp_c[64:128, 1:2]).then_inc(next_ready, 1)

            def high_part(b, w):
                act.wait_ge((qk01_done, qk2_done)[w], b.n + 1)
                if later(b, 1):
                    act.wait_ge(parts_out[w], 16 * b.n)
                for i in range((2, 1)[w]):
                    m = 2 * w + i
                    last = fn(parts[w][:, i, 0, :], (ps_y, ps_z)[w][:, i * NTOK:(i + 1) * NTOK],
                              ACT.Identity, bias=bqk_c[:, m:m + 1])
                last.then_inc((qk01_high, qk2_high)[w], 1)

            def step(b, first=False, early=False, project_next=True):
                ahead = nxt(nxt(b))
                if not first:
                    attention_out(prv(b), fresh=early)
                sigmoid(b, 0, first)
                sigmoid(b, 1, first)
                sigmoid(b, 2, first)
                if project_next:
                    h_out(ahead)
                sigmoid(b, 3, first)
                if project_next and ahead.par == 0:
                    next_h_out(ahead)
                sigmoid(b, 4, first)
                sigmoid(b, 5, first)
                if project_next:
                    high_part(ahead, 0)
                    high_part(ahead, 1)

            act.wait_ge(emb_in, 32)
            for n in range(2):
                h_out(at(n))
                if n == 0:
                    next_h_out(at(n))
                    act.wait_ge(qk_in, 32)
                high_part(at(n), 0)
                high_part(at(n), 1)
            act.wait_ge(const_in, CONSTS)
            step(at(0), first=True)
            step(at(1), early=True)
            step(at(2))
            with act.Fori(1, NB // 2 - 2) as i:
                step(At(2 * i + 1, i, 1))
                step(At(2 * i + 2, i + 1, 0))
            step(at(NB - 3))
            step(at(NB - 2), project_next=False)
            step(at(NB - 1), project_next=False)
            attention_out(at(NB - 1))

            act.wait_ge(slots_dve, 1)
            fn(slot_s[:, 1:2], slot_s[:, 0:1], ACT.Sqrt).then_inc(tables_act, 1)
            act.wait_ge(kept, 3 * NB)
            fn(lcoef, mv[:, :, 1], ACT.Sqrt, bias=eps_c).then_inc(tables_act, 1)
            fn(ssu, ssu, ACT.Sqrt).then_inc(tables_act, 1)
            act.wait_ge(tables_dve, 4)
            fn(lcoef, tmp, ACT.Sqrt, bias=eps_c).then_inc(tables_act, 1)

            def normalise(p):
                if later(p, 4):
                    act.wait_ge(y_done, p.n - 3)
                    act.wait_ge(h1_kept, p.n - 3)
                for t in range(TT):
                    row = bass.ds(4 * p.n + t, 1)
                    last = fn(h1s[p.ring][:, 0, t, :], res[:, row, :].rearrange("p a d -> p (a d)"),
                              ACT.Identity, bias=nmr[:, row], scale=rstd[:, row])
                last.then_inc(h1_ready[0], 1)

            def hT2_out(p):
                for u in range(2):
                    act.wait_ge(hT2_done, 2 * p.n + u + 1)
                    if u == 0 and later(p, 2):
                        act.wait_ge(lg_done, p.n - 1)
                    last = fn(hT2[p.par][:, u].rearrange("p k n -> p (k n)"), bank(u)[0:KP, 0:KT * NTOK],
                              ACT.Identity)
                last.then_inc(hT2_ready, 1)

            def exp_slots(p):
                act.wait_ge(zm_ready, p.n + 1)
                fn(ez[p.par], ez[p.par], ACT.Exp).then_inc(ez_ready, 1)

            def exp_tokens(p):
                act.wait_ge(nmt_ready, p.n + 1)
                if later(p, 2):
                    act.wait_ge(d_done, p.n - 1)
                    act.wait_ge(rzt_ready, p.n - 1)
                fn(pt[p.par], zs[p.par], ACT.Exp, bias=nmt[p.par], accum_out=zt[p.par]).then_inc(pt_ready, 1)

            def comb_out(p):
                act.wait_ge(e_done, p.n + 1)
                fn(comb[:, bass.ds(p.n, 1), :].rearrange("p a n -> p (a n)"),
                   bank(5)[:, 0:NTOK], ACT.Copy).then_inc(comb_ready, 1)

            def y_out(p):
                act.wait_ge(y_done, p.n + 1)
                act.wait_ge(rzt_ready, p.n + 1)
                if later(p, 2):
                    act.wait_ge(yT_done, p.n - 1)
                fn(ys[p.par], bank(6)[:, 0:D], ACT.Copy, scale=rzt[p.par]).then_inc(ys_ready, 1)

            def yT_out(p):
                act.wait_ge(yT_done, p.n + 1)
                for k in range(KT):
                    last = fn(yT[:, k, bass.ds(2 * p.n, 2), :].rearrange("p u s -> p (u s)"),
                              bank(7)[0:KP, 2 * NS * k:2 * NS * (k + 1)], ACT.Copy, scale=nw_c[:, k:k + 1])
                last.then_inc(yT_ready, 1)

            def act_step(s):
                for lag, stage in ((2, exp_slots), (3, comb_out), (4, yT_out), (0, hT2_out), (1, exp_tokens),
                                   (3, y_out), (-1, normalise)):
                    if s.has(lag):
                        stage(s.back(lag))

            route(act, act_step)

            def gelu(j):
                act.wait_ge(fc1_done, j.n + 1)
                if later(j, 1):
                    act.wait_ge(hidT_done, j.n)
                fn(hid.rearrange("p (h f) -> p h f", h=2),
                   bank(2 * j.par, 2).rearrange("p (h f) -> p h f", h=2)[:, :, 0:F // 2],
                   ACT.Gelu).then_inc(hid_ready, 1)

            gelu(at(0))
            with act.Fori(0, NPAIR // 2 - 1) as i:
                gelu(At(2 * i + 1, i, 1))
                gelu(At(2 * i + 2, i + 1, 0))
            gelu(at(NPAIR - 1))

            def root(i):
                act.wait_ge(mv4_ready, i.n + 1)
                fn(sd4[i.ring], mv4[i.ring][:, :, 1], ACT.Sqrt, bias=eps_c).then_inc(sd4_ready, 1)

            def final(i):
                act.wait_ge(nm4_ready, i.n + 1)
                if later(i, RING):
                    act.wait_ge(out_done[i.ring], 16 * i.turn)
                for t in range(4):
                    last = fn(ob[i.ring][:, t, :], rf[i.ring][:, t, :], ACT.Identity,
                              bias=nm4[i.ring][:, t:t + 1], scale=rs4[i.ring][:, t:t + 1])
                last.then_inc(ob_ready, 1)
                act.wait_ge(ob_ready, i.n + 1)
                act.dma_start(out_v[:, bass.ds(4 * i.n, 4), :], ob[i.ring]).then_inc(out_done[i.ring], 16)

            root(ringed(0, 0))
            for u in range(1, RING + 1):
                root(ringed(0, u))
                final(ringed(0, u - 1))
            with act.Fori(1, NPAIR // RING - 1) as i:
                for u in range(1, RING + 1):
                    root(ringed(i, u))
                    final(ringed(i, u - 1))
            for u in range(1, RING):
                root(ringed(NPAIR // RING - 1, u))
                final(ringed(NPAIR // RING - 1, u - 1))
            final(ringed(NPAIR // RING - 1, RING - 1))

        @block.gpsimd
        def _(pool):
            copy = nc.gpsimd.tensor_copy
            nc.gpsimd.memset(eps_c, EPS)
            for v in vz:
                last = nc.gpsimd.memset(v, 0.0)
            last.then_inc(vz_zero, 1)

            def keep_rows(b):
                pool.wait_ge(r_ready, b.n + 1)
                copy(res[:, bass.ds(2 * b.n, 2), :], rt[b.par]).then_inc(kept, 1)
                pool.wait_ge(mv_ready, b.n + 1)
                copy(mv[:, bass.ds(2 * b.n, 2), :], mvt[b.par]).then_inc(kept, 1)
                pool.wait_ge(ss_ready, b.n + 1)
                copy(ssu[:, bass.ds(2 * b.n, 2)], sst[b.par]).then_inc(kept, 1)

            with pool.Fori(0, NB // 2) as i:
                keep_rows(At(2 * i, i, 0))
                keep_rows(At(2 * i + 1, i, 1))

            with pool.Fori(0, NPAIR // RING) as i:
                for u in range(RING):
                    for s in h1_ready:
                        pool.wait_ge(s, RING * i + u + 1)
                    copy(res[:, bass.ds(2 * TT * (RING * i + u), 2 * TT), :],
                         h1s[u].rearrange("p u t d -> p (u t) d")).then_inc(h1_kept, 1)

            pool.wait_ge(yT_ready, NPAIR)
            pool.wait_ge(comb_ready, NPAIR)
            pool.wait_ge(h1_kept, NPAIR)
            for n, y in enumerate(yst):
                nc.gpsimd.memset(y[KP:KP + 1], 1.0).then_inc(ones_set, 1)
                pool.wait_ge(ones_set, n + 1)

            def stage_y(j, fresh=False):
                if not fresh:
                    pool.wait_ge(fc1_done, j.n - 1)
                for k in range(KT):
                    last = copy(yst[j.par][0:KP, k], yT[:, k, :, bass.ds(2 * j.n, 2)].rearrange("p b s -> p s b"))
                last.then_inc(yst_ready, 1)

            stage_y(at(0), True)
            stage_y(at(1), True)
            with pool.Fori(1, NPAIR // 2) as i:
                stage_y(At(2 * i, i, 0))
                stage_y(At(2 * i + 1, i, 1))

            def stage_c(i):
                if later(i, RING):
                    pool.wait_ge(cm_done, i.n - RING + 1)
                copy(cst[i.ring], comb[:, bass.ds(i.n, 1), :].rearrange("p a n -> p (a n)")).then_inc(cst_ready, 1)
                pool.wait_ge(y2_in[i.ring], 32 * (i.turn + 1))
                nc.gpsimd.tensor_tensor(y2s[i.ring], y2s[i.ring], b2_s, ALU.add).then_inc(y2_biased, 1)

            pool.wait_ge(fc1_done, NPAIR)
            pool.wait_ge(yst_ready, NPAIR)
            pool.wait_ge(b2_in, 32)
            for u in range(RING):
                stage_c(ringed(0, u))
            with pool.Fori(1, NPAIR // RING) as i:
                for u in range(RING):
                    stage_c(ringed(i, u))

        @block.vector
        def _(dve):
            v = nc.vector

            def rests(b, w):
                done, ready = (qk01_high, qk2_high)[w], (qk01_rest, qk2_rest)[w]
                dve.wait_ge(done, b.n + 1)
                if later(b, 1):
                    dve.wait_ge((qk01_parts, qk2_parts)[w], b.n)
                for i in range((2, 1)[w]):
                    m = 2 * w + i
                    last = v.scalar_tensor_tensor(out=rest[w][:, i, :],
                                                  in0=(ps_y, ps_z)[w][:, i * NTOK:(i + 1) * NTOK],
                                                  scalar=bqk_c[:, m:m + 1], in1=parts[w][:, i, 0, :],
                                                  op0=ALU.add, op1=ALU.subtract)
                last.then_inc(ready, 1)

            def middle_part(b, w):
                dve.wait_ge((qk01_rest, qk2_rest)[w], b.n + 1)
                v.tensor_copy(parts[w][:, :, 1, :], rest[w]).then_inc((qk01_mid, qk2_mid)[w], 1)

            def low_part(b, w):
                dve.wait_ge((qk01_mid, qk2_mid)[w], b.n + 1)
                v.tensor_tensor(parts[w][:, :, 2, :], rest[w], parts[w][:, :, 1, :], ALU.subtract
                                ).then_inc((qk01_parts, qk2_parts)[w], 1)

            def v_out(b):
                dve.wait_ge(v_done, b.n + 1)
                if later(b, 2):
                    dve.wait_ge(av_done, 2 * b.n - 2)
                dst = vz[b.par].rearrange("p t (g a) f -> p (t g) a f", a=4)[:, :, 0:4:3, :]
                v.tensor_tensor(dst, ps_x[0:TP, 0:TT * D].rearrange("p (g a f) -> p g a f", a=2, f=HD),
                                bv_b.rearrange("p t (g a f) -> p (t g) a f", a=2, f=HD),
                                ALU.add).then_inc(v_ready, 1)

            def h_rows(b):
                dve.wait_ge(tr_done, b.n + 1)
                if later(b, 2):
                    dve.wait_ge(r_ready, b.n - 1)
                v.tensor_tensor(hb[b.par], tiles(ps_z, TP, D), bo_b, ALU.add).then_inc(hb_ready, 1)

            def residual(b, early=False):
                dve.wait_ge(o_done, b.n + 1)
                dve.wait_ge(hb_ready, b.n + 1)
                if not early:
                    dve.wait_ge(kept, 3 * b.n - 3)
                v.tensor_tensor(rt[b.par], tiles(ps_y, TP, D), hb[b.par], ALU.add).then_inc(r_ready, 1)

            def finish(b):
                dve.wait_ge(r_ready, b.n + 1)
                for t in range(TT):
                    last = v.bn_stats(st[:, t, :], rt[b.par][:, t, :])
                last.then_inc(st_ready, 1)
                apart(dve, vz_zero, 1)
                dve.wait_ge(st_ready, b.n + 1)
                for t in range(TT):
                    last = v.bn_aggr(mvt[b.par][:, t, :], st[:, t, :])
                last.then_inc(mv_ready, 1)
                dve.wait_ge(mv_ready, b.n + 1)
                for t in range(TT):
                    last = v.scalar_tensor_tensor(out=ut[:, t, :], in0=rt[b.par][:, t, :],
                                                  scalar=mvt[b.par][:, t, 0:1], in1=nw_b[:, t, :],
                                                  op0=ALU.subtract, op1=ALU.mult)
                last.then_inc(u_ready, 1)
                dve.wait_ge(u_ready, b.n + 1)
                for t in range(TT):
                    last = v.tensor_tensor_reduce(out=ut[:, t, :], in0=ut[:, t, :], in1=ut[:, t, :], scale=1.0,
                                                  scalar=0.0, op0=ALU.mult, op1=ALU.add,
                                                  accum_out=sst[b.par][:, t:t + 1])
                last.then_inc(ss_ready, 1)
                dve.wait_ge(ss_ready, b.n + 1)

            def make_parts(b, values=True):
                rests(b, 0)
                middle_part(b, 0)
                rests(b, 1)
                low_part(b, 0)
                if values:
                    v_out(b)
                middle_part(b, 1)
                low_part(b, 1)

            def step(b, first=False, early=False, project_next=True, value_next=True):
                if not first:
                    residual(prv(b), early=early)
                if value_next:
                    h_rows(nxt(b))
                if not first:
                    finish(prv(b))
                if project_next:
                    make_parts(nxt(nxt(b)))

            dve.wait_ge(qk_in, 32)
            for n in range(2):
                make_parts(at(n), values=False)
            dve.wait_ge(const_in, CONSTS)
            dve.wait_ge(vz_zero, 1)
            v_out(at(0))
            h_rows(at(0))
            v_out(at(1))
            step(at(0), first=True)
            step(at(1), early=True)
            step(at(2), early=True)
            with dve.Fori(1, NB // 2 - 2) as i:
                step(At(2 * i + 1, i, 1))
                step(At(2 * i + 2, i + 1, 0))
            step(at(NB - 3))
            step(at(NB - 2), project_next=False)
            step(at(NB - 1), project_next=False, value_next=False)

            def table(ins, sem, made):
                ins.then_inc(sem, 1)
                dve.wait_ge(sem, made)

            def rooted(n):
                dve.wait_ge(tables_act, n)

            table(v.tensor_tensor_reduce(out=slot_sq, in0=slot_rows, in1=slot_rows, scale=1.0, scalar=0.0,
                                         op0=ALU.mult, op1=ALU.add, accum_out=slot_s[:, 0:1]), slots_dve, 1)
            rooted(1)
            table(v.tensor_scalar(slot_s[:, 1:2], slot_s[:, 1:2], EPS, None, ALU.max), slots_dve, 2)
            table(v.reciprocal(slot_s[:, 2:3], slot_s[:, 1:2]), slots_dve, 3)
            table(v.tensor_scalar(slot_sq, slot_rows, slot_s[:, 2:3], slot_s[:, 3:4], ALU.mult, ALU.mult),
                  slots_dve, SLOTS_AT)
            residual(at(NB - 1))
            finish(at(NB - 1))
            dve.wait_ge(slT_done, 1)
            for k in range(KT):
                last = v.tensor_scalar(slwT[:, k, :], ps_y[0:KP, k * NS:(k + 1) * NS], nw_c[:, k:k + 1], None,
                                       ALU.mult)
            last.then_inc(slwT_ready, 1)

            rooted(2)
            table(v.reciprocal(rstd, lcoef), tables_dve, 1)
            table(v.scalar_tensor_tensor(out=nmr, in0=mv[:, :, 0], scalar=-1.0, in1=rstd, op0=ALU.mult,
                                         op1=ALU.mult), tables_dve, 2)
            table(v.tensor_tensor(tmp, rstd, rstd, ALU.mult), tables_dve, 3)
            table(v.tensor_tensor(tmp, tmp, mv[:, :, 1], ALU.mult), tables_dve, 4)
            rooted(3)
            table(v.tensor_tensor(ssu, ssu, rstd, ALU.mult), tables_dve, 5)
            rooted(4)
            table(v.reciprocal(rms, lcoef), tables_dve, 6)
            table(v.tensor_tensor(ssu, ssu, rms, ALU.mult), tables_dve, 7)
            table(v.tensor_scalar(ssu, ssu, EPS, None, ALU.max), tables_dve, 8)
            table(v.reciprocal(tmp, ssu), tables_dve, 9)
            table(v.tensor_tensor(lcoef, tmp, rms, ALU.mult), tables_dve, LCOEF_AT)
            dve.wait_ge(lcT_done, 1)
            v.tensor_copy(lcT, ps_z[0:NB * TT, 0:TP]).then_inc(lcT_ready, 1)

            def normalise(p):
                if later(p, 4):
                    dve.wait_ge(y_done, p.n - 3)
                    dve.wait_ge(h1_kept, p.n - 3)
                for t in range(TT):
                    row = bass.ds(4 * p.n + TT + t, 1)
                    last = v.tensor_scalar(h1s[p.ring][:, 1, t, :], res[:, row, :].rearrange("p a d -> p (a d)"),
                                           rstd[:, row], nmr[:, row], ALU.mult, ALU.add)
                last.then_inc(h1_ready[1], 1)

            def logits_waits(p):
                dve.wait_ge(lg_done, p.n + 1)
                dve.wait_ge(lc_in[p.par], 32 * p.half + 32)
                if later(p, 2):
                    dve.wait_ge(zr_done, p.n - 1)

            def logits_out(p):
                v.tensor_tensor_reduce(out=zs[p.par], in0=bank(2)[:, 0:NTOK], in1=lcb[p.par], scale=1.0,
                                       scalar=LOWEST, op0=ALU.mult, op1=ALU.max,
                                       accum_out=mxt[p.par]).then_inc(zs_ready, 1)
                dve.wait_ge(zs_ready, p.n + 1)
                v.tensor_scalar(nmt[p.par], mxt[p.par], -1.0, None, ALU.mult).then_inc(nmt_ready, 1)

            def slot_max(p):
                dve.wait_ge(zr_done, p.n + 1)
                rows = bank(3)[0:TP, 0:TT * 2 * NS].rearrange("p (g s) -> p g s", s=NS)
                v.tensor_reduce(mx2, rows, AX_X, ALU.max).then_inc(mx_ready, 1)
                dve.wait_ge(mx_ready, p.n + 1)
                if later(p, 2):
                    dve.wait_ge(e_done, p.n - 1)
                v.tensor_tensor(ez[p.par].rearrange("p t (u s) -> p (t u) s", s=NS), rows,
                                mx2.unsqueeze(2).to_broadcast([TP, TT * 2, NS]), ALU.subtract
                                ).then_inc(zm_ready, 1)

            def over_slots(p):
                dve.wait_ge(ez_ready, p.n + 1)
                e = ez[p.par].rearrange("p t (u s) -> p (t u) s", s=NS)
                v.tensor_reduce(sm2, e, AX_X, ALU.add).then_inc(sm_ready, 1)
                dve.wait_ge(sm_ready, p.n + 1)
                v.reciprocal(rc2, sm2).then_inc(rc_ready, 1)
                dve.wait_ge(rc_ready, p.n + 1)
                v.tensor_tensor(e, e, rc2.unsqueeze(2).to_broadcast([TP, TT * 2, NS]),
                                ALU.mult).then_inc(en_ready, 1)

            def token_sum(p):
                dve.wait_ge(pt_ready, p.n + 1)
                if later(p, 2):
                    dve.wait_ge(ys_ready, p.n - 1)
                v.reciprocal(rzt[p.par], zt[p.par]).then_inc(rzt_ready, 1)

            def dispatch_rows(p):
                dve.wait_ge(d_done, p.n + 1)
                if later(p, 2):
                    dve.wait_ge(y_done, p.n - 1)
                factor = rms[:, bass.ds(4 * p.n, 4)].rearrange("p (u t) -> p t u", t=TT)
                v.tensor_tensor(dr[p.par], bank(4)[0:TP, 0:TT * 2 * NS].rearrange("p (t u s) -> p t u s", t=TT, s=NS),
                                factor.unsqueeze(3).to_broadcast([TP, TT, 2, NS]),
                                ALU.mult).then_inc(dr_ready, 1)

            def dve_step(s):
                for lag, stage in ((3, dispatch_rows), (1, logits_waits), (2, token_sum), (1, logits_out),
                                   (2, over_slots),
                                   (-1, normalise), (1, slot_max)):
                    if s.has(lag):
                        stage(s.back(lag))

            route(dve, dve_step)

            def hidden_out(j):
                dve.wait_ge(hidT_done, j.n + 1)
                if later(j, 1):
                    dve.wait_ge(fc2_done, j.n)
                v.tensor_copy(hidT, bank(4, 2)[:, 0:F].rearrange("p (k n) -> p k n", k=FK)
                              ).then_inc(hidT_ready, 1)

            def y2_rows(j, fresh=False):
                dve.wait_ge(fc2_done, j.n + 1)
                if not fresh:
                    dve.wait_ge(y2_out[j.par], 16 * j.half)
                v.tensor_copy(y2o[j.par], bank(6)[:, 0:D]).then_inc(y2_ready, 1)

            def expert(j, fresh=False):
                hidden_out(j)
                y2_rows(j, fresh)

            expert(at(0), True)
            expert(at(1), True)
            with dve.Fori(1, NPAIR // 2) as i:
                expert(At(2 * i, i, 0))
                expert(At(2 * i + 1, i, 1))

            def pair(i, first=False, last=False):
                if not last:
                    dve.wait_ge(cm_done, i.n + 1)
                    v.tensor_tensor(rf[i.ring].rearrange("p (e t) d -> p e (t d)", e=2),
                                    bank(2 * i.ring, 2).rearrange("p (e n) -> p e n", e=2)[0:TP, :, 0:TT * D],
                                    res[:, bass.ds(4 * i.n, 4), :].rearrange("p (e t) d -> p e (t d)", e=2),
                                    ALU.add).then_inc(rf_ready, 1)
                if not first:
                    ring = (i.ring - 1) % RING
                    dve.wait_ge(sd4_ready, i.n)
                    v.reciprocal(rs4[ring], sd4[ring]).then_inc(rs4_ready, 1)
                if not last:
                    dve.wait_ge(rf_ready, i.n + 1)
                    for t in range(4):
                        last_op = v.bn_stats(st4[:, t, :], rf[i.ring][:, t, :])
                    last_op.then_inc(st4_ready, 1)
                if not first:
                    dve.wait_ge(rs4_ready, i.n)
                    v.scalar_tensor_tensor(out=nm4[ring], in0=mv4[ring][:, :, 0], scalar=-1.0, in1=rs4[ring],
                                           op0=ALU.mult, op1=ALU.mult).then_inc(nm4_ready, 1)
                if not last:
                    apart(dve, vz_zero, 1)
                    dve.wait_ge(st4_ready, i.n + 1)
                    for t in range(4):
                        last_op = v.bn_aggr(mv4[i.ring][:, t, :], st4[:, t, :])
                    last_op.then_inc(mv4_ready, 1)

            dve.wait_ge(yst_ready, NPAIR)
            for u in range(RING):
                pair(ringed(0, u), first=u == 0)
            with dve.Fori(1, NPAIR // RING) as i:
                for u in range(RING):
                    pair(ringed(i, u))
            pair(ringed(NPAIR // RING, 0), last=True)


def kernel(**inputs):
    import numpy as np
    import concourse.bacc as bacc
    from concourse.bass_utils import run_bass_kernel_spmd

    a = {k: np.asarray(val) for k, val in inputs.items()}
    side, p = a["x"].shape[2] // 16, 16

    def rows(w, tiles):
        return w.reshape(tiles, w.shape[0] // tiles, -1).transpose(1, 0, 2)

    def by_head(w):
        return w.reshape(-1, MT, 1, HPT, HD).transpose(0, 1, 2, 4, 3)

    w1 = a["L0_ffn_fc1_weight"].reshape(NS, KT, KP, 2, F // 2)
    b1 = np.zeros((NS, 2, 1, KT, F // 2), w1.dtype)
    b1[:, :, 0, KT - 1] = a["L0_ffn_fc1_bias"].reshape(NS, 2, F // 2)

    turned = np.r_[0:KP, D - (128 - KP):D, KP:D - (128 - KP)]
    bp = a["L0_tok_bp"][turned]

    wo = a["L0_attn_Wo"].T
    strips = np.concatenate([np.arange(32 * g, 32 * g + 32) for g in (0, 1, 2, 3, 4, 4, 5, 5)])
    x = a["x"].reshape(NB, 3, side, p, side, p).transpose(0, 1, 3, 5, 2, 4)
    arrays = {
        "x": x.reshape(NB, PK, 128, NTOK).transpose(0, 2, 1, 3),
        "wp": rows(a["L0_tok_Wp"].T[:, turned], PK),
        "bp": np.stack([bp[0:128], np.concatenate([bp[128:D], bp[128:D]])], axis=1),
        "attn_bias": a["L0_attn_bias"].reshape(1, 1),
        "wqk": rows(np.concatenate([by_head(a["L0_attn_Wq"].T), by_head(a["L0_attn_Wk"].T)], axis=2
                                   ).reshape(D, MT * 128), KT),
        "bqk": np.concatenate([by_head(a["L0_attn_bq"].reshape(1, D)), by_head(a["L0_attn_bk"].reshape(1, D))],
                              axis=2).reshape(MT, 128).T,
        "wv": rows(a["L0_attn_Wv"].T, KT),
        "bv": a["L0_attn_bv"],
        "wo": wo[strips].reshape(2, 128, D).transpose(1, 0, 2),
        "bo": a["L0_attn_bo"],
        "slots": a["L0_ffn_slots"],
        "scale": a["L0_ffn_scale"].reshape(NS, 1),
        "w1": np.concatenate([w1.transpose(0, 3, 2, 1, 4), b1], axis=2),
        "w2": a["L0_ffn_fc2_weight"].reshape(NS, FK, 128, D).transpose(0, 2, 1, 3),
        "b2": a["L0_ffn_fc2_bias"],
        "norm_w": a["L0_ffn_norm_weight"],
        "norm_c": a["L0_ffn_norm_weight"].reshape(KT, KP).T,
        "ident": np.eye(128, dtype=np.float32),
    }
    nc = bacc.Bacc("TRN2", target_bir_lowering=False, num_devices=1)
    feeds, aps = {}, []
    for name, arr in arrays.items():
        arr = np.ascontiguousarray(arr)
        feeds[f"in_{name}"] = arr
        aps.append(nc.dram_tensor(f"in_{name}", arr.shape, mybir.dt.from_np(arr.dtype), kind="ExternalInput").ap())
    out = nc.dram_tensor("out", (NB, NTOK, D), F32, kind="ExternalOutput").ap()
    vit_tower(nc, *aps, out)
    r = run_bass_kernel_spmd(nc, [feeds], core_ids=[0])
    return r.results[0]["out"]
```
